# Optimizing a Trainium2 kernel written in Bass

```python
import numpy as np
import jax
import jax.numpy as jnp

def _softmax(x, axis=-1):
    return jax.nn.softmax(x, axis=axis)

def _gelu(x):
    return jax.nn.gelu(x, approximate=True)

def _silu(x):
    return jax.nn.silu(x)

def _sigmoid(x):
    return jax.nn.sigmoid(x)

def _layernorm(x, axis=-1, eps=1e-05):
    m = jnp.mean(x, axis=axis, keepdims=True)
    v = jnp.var(x, axis=axis, keepdims=True)
    return (x - m) / jnp.sqrt(v + eps)

def _scatter_add(tgt, idx, src, axis=0):
    return tgt.at[idx].add(src)

def _segment_sum(src, seg, n):
    return jax.ops.segment_sum(src, seg, n)
kernel_name = 'mk_flamingo_gated_d1_seqx_r8_f64d92'

def setup_inputs(seed: int=0):
    np.random.seed(seed)
    _w = jnp.asarray

    def _rec_inputs():
        import jax
        import jax.numpy as jnp
        _rk = jax.random.key(seed)
        x = 7.22e-05 + 1 * jax.random.normal(jax.random.fold_in(_rk, 1), (32, 128, 128), jnp.float32)
        _lenS = 128 - jax.random.randint(jax.random.fold_in(_rk, 7), (32,), 0, max(1, 128 // 4) + 1, jnp.int32)
        _lenS2 = 128 - jax.random.randint(jax.random.fold_in(_rk, 8), (32,), 0, max(1, 128 // 4) + 1, jnp.int32)
        itok_S_0_31 = jax.random.randint(jax.random.fold_in(_rk, 11), (128,), 0, 32, jnp.int32)
        _ctx_1024P = jax.random.normal(jax.random.fold_in(_rk, 12), (32, 16, 128), jnp.float32)
        _ctx_1024c = jax.random.dirichlet(jax.random.fold_in(_rk, 512), 0.3 * jnp.ones((16,), jnp.float32), (32, 128))
        _ctx_1024t = jnp.einsum('bsk,bkd->bsd', _ctx_1024c, _ctx_1024P)
        _ctx_1024t = _ctx_1024t * jax.lax.rsqrt(jnp.mean(jnp.square(_ctx_1024t)) + 1e-12) * 0.953939
        ctx_1024 = 0.000121155 + 1.00018 * (_ctx_1024t + 0.3 * jax.random.normal(jax.random.fold_in(_rk, 612), (32, 128, 128), jnp.float32))
        _g = jax.random.normal(jax.random.fold_in(_rk, 9001), (2, 1), jnp.float32)
        _g = jnp.sign(_g) * jnp.maximum(jnp.abs(_g), 1.0) + (_g == 0) * 1.0
        g_xattn = _g[0]
        g_ffn = _g[1]
        return (x, itok_S_0_31, ctx_1024, g_xattn, g_ffn)
    x, itok_S_0_31, ctx_1024, g_xattn, g_ffn = _rec_inputs()

    def _L0_xattn_setup():
        import jax, jax.numpy as jnp
        import numpy as np
        NUM_LAYERS = 32
        IN_SIZE = 128
        OUT_SIZE = 128
        B, S = (32, 32)
        key = jax.random.key(seed)
        k1, k2, k3 = jax.random.split(key, 3)
        x = jax.random.normal(k1, (B, S, IN_SIZE), dtype=jnp.float32)
        layer_idx = jax.random.randint(k2, (S,), 0, NUM_LAYERS, dtype=jnp.int32)
        weight = jax.random.normal(k3, (NUM_LAYERS, OUT_SIZE, IN_SIZE), dtype=jnp.float32)
        return {'x': x, 'layer_idx': layer_idx, 'weight': weight}
    _L0_xattn_all = _L0_xattn_setup()
    _L0_xattn_in = {k: v for k, v in _L0_xattn_all.items() if k in ()}
    del _L0_xattn_all

    def _L0_ffn_setup():
        import jax, jax.numpy as jnp
        import numpy as np
        B, L, D = (2, 256, 128)
        E = 15
        H = D * 1
        K = 3
        T = 1.0
        key = jax.random.key(seed)
        ks = jax.random.split(key, 12)
        s = 0.02
        return {'x': jax.random.normal(ks[0], (B, L, D), dtype=jnp.float32), 'router_W': jax.random.normal(ks[1], (D, E), dtype=jnp.float32) * s, 'router_b': jnp.zeros((E,), dtype=jnp.float32), 'sW1': jax.random.normal(ks[2], (D, H), dtype=jnp.float32) * s, 'sb1': jnp.zeros((H,), dtype=jnp.float32), 'sW2': jax.random.normal(ks[3], (H, D), dtype=jnp.float32) * s, 'sb2': jnp.zeros((D,), dtype=jnp.float32), 'eW1': jax.random.normal(ks[4], (E, D, H), dtype=jnp.float32) * s, 'eb1': jnp.zeros((E, H), dtype=jnp.float32), 'eW2': jax.random.normal(ks[5], (E, H, D), dtype=jnp.float32) * s, 'eb2': jnp.zeros((E, D), dtype=jnp.float32)}
    _L0_ffn_all = _L0_ffn_setup()
    _L0_ffn_in = {k: v for k, v in _L0_ffn_all.items() if k in ('router_W', 'router_b', 'sW1', 'sb1', 'sW2', 'sb2', 'eW1', 'eb1', 'eW2', 'eb2')}
    del _L0_ffn_all
    return {'x': x, 'itok_S_0_31': itok_S_0_31, 'ctx_1024': ctx_1024, 'g_xattn': g_xattn, 'g_ffn': g_ffn, 'L0_ffn_router_W': _L0_ffn_in['router_W'], 'L0_ffn_router_b': _L0_ffn_in['router_b'], 'L0_ffn_sW1': _L0_ffn_in['sW1'], 'L0_ffn_sb1': _L0_ffn_in['sb1'], 'L0_ffn_sW2': _L0_ffn_in['sW2'], 'L0_ffn_sb2': _L0_ffn_in['sb2'], 'L0_ffn_eW1': _L0_ffn_in['eW1'], 'L0_ffn_eb1': _L0_ffn_in['eb1'], 'L0_ffn_eW2': _L0_ffn_in['eW2'], 'L0_ffn_eb2': _L0_ffn_in['eb2']}

def reference(x, itok_S_0_31, ctx_1024, g_xattn, g_ffn, L0_ffn_router_W, L0_ffn_router_b, L0_ffn_sW1, L0_ffn_sb1, L0_ffn_sW2, L0_ffn_sb2, L0_ffn_eW1, L0_ffn_eb1, L0_ffn_eW2, L0_ffn_eb2):
    import jax
    import jax.numpy as jnp

    def _L0_xattn_ref(x, layer_idx, weight):
        import jax, jax.numpy as jnp
        import numpy as np
        NUM_LAYERS = 32
        IN_SIZE = 128
        OUT_SIZE = 128
        B, S = (32, 32)
        w = weight[layer_idx]
        return jnp.einsum('bsd,sod->bso', x, w)

    def _L0_ffn_ref(x, router_W, router_b, sW1, sb1, sW2, sb2, eW1, eb1, eW2, eb2):
        import jax, jax.numpy as jnp
        import numpy as np
        B, L, D = (2, 256, 128)
        E = 15
        H = D * 1
        K = 3
        T = 1.0
        b, l, d = x.shape
        n = b * l
        xt = x.reshape(n, d)
        shared = jax.nn.relu(xt @ sW1 + sb1) @ sW2 + sb2
        logits = xt @ router_W + router_b
        probs = jax.nn.softmax(logits / T, axis=-1)
        top_p, top_i = jax.lax.top_k(probs, K)
        cw = jnp.zeros((n, E), dtype=probs.dtype)
        cw = cw.at[jnp.arange(n)[:, None], top_i].set(top_p)
        h = jax.nn.relu(jnp.einsum('nd,edh->neh', xt, eW1) + eb1)
        ye = jnp.einsum('neh,ehd->ned', h, eW2) + eb2
        routed = jnp.einsum('ned,ne->nd', ye, cw)
        return (shared + routed).reshape(b, l, d)
    x = x + jnp.tanh(g_xattn[0]) * _L0_xattn_ref(_layernorm(x, axis=-1), itok_S_0_31, ctx_1024)
    x = x + jnp.tanh(g_ffn[0]) * _L0_ffn_ref(_layernorm(x, axis=-1), L0_ffn_router_W, L0_ffn_router_b, L0_ffn_sW1, L0_ffn_sb1, L0_ffn_sW2, L0_ffn_sb2, L0_ffn_eW1, L0_ffn_eb1, L0_ffn_eW2, L0_ffn_eb2)
    return x

_drawn_inputs = setup_inputs


def setup_inputs(seed=0):
    import zlib

    import numpy as np

    out = dict(_drawn_inputs(seed))
    spreads = {'L0_ffn_router_b': (0.0, 0.8),
     'L0_ffn_sb1': (0.0, 0.8),
     'L0_ffn_sb2': (0.0, 0.661),
     'L0_ffn_eb1': (0.0, 0.8),
     'L0_ffn_eb2': (0.0, 0.8)}
    factors = {'L0_ffn_router_W': 8.0,
     'L0_ffn_sW1': 8.0,
     'L0_ffn_sW2': 8.0,
     'L0_ffn_eW1': 8.0,
     'L0_ffn_eW2': 8.0}
    for name, (base, spread) in spreads.items():
        noise = np.random.default_rng([zlib.crc32(name.encode()), seed]).standard_normal(out[name].shape)
        drawn = base * np.exp(spread * noise) if base else spread * noise
        out[name] = jnp.asarray(drawn.astype(out[name].dtype))
    for name, factor in factors.items():
        out[name] = (out[name] * factor).astype(out[name].dtype)
    return out
```

```python
import numpy as np
import concourse.bass as bass
from concourse import mybir
from contextlib import ExitStack

F32 = mybir.dt.float32
F32R = mybir.dt.float32r
I32 = mybir.dt.int32
ALU = mybir.AluOpType
ACT = mybir.ActivationFunctionType
AX = mybir.AxisListType

EPS = 1e-5
TOPK = 3


def count(chunk, per, plus=0):
    k, r = chunk
    return k * (2 * per) + (r * per + plus)


def count_slot(chunk, per):
    k, r = chunk
    return k * per + ((r // 2 + 1) * per)


def held(eng, name, value):
    if isinstance(value, int):
        return value
    reg = eng.alloc_register(name)
    eng.reg_mov(reg, value)
    return reg


def before(chunk, n=1):
    return (chunk[0], chunk[1] - n)


def after(chunk):
    return (chunk[0], chunk[1] + 1)


def gated_moe_block(nc, x, itok, ctx_w, g_xattn, g_ffn, router_W, router_b, sW1, sb1, sW2, sb2,
                    eW1, eb1, eW2, eb2, out):
    NB, S, D = x.shape
    NMAT = ctx_w.shape[0]
    E = router_W.shape[1]
    NE = E + 1
    Q = 4
    TI = 4
    CS = Q * TI
    C = CS * NB
    NCHUNK = S // CS
    P = 128
    H = sW1.shape[1]
    assert D == P and H == P and NB == 32 and NCHUNK % 2 == 0
    NZ = 4
    NT = 4
    LAG = 3
    CG = 4
    GROUP = [range(0, 3), range(3, 7), range(7, 11), range(11, 15)]
    PADK = TOPK + 5
    EW = E + 5

    POOL_LO = [u for u in range(NE) if u % 3 != 1]
    DVE_LO = [u for u in range(NE) if u % 3 == 1]

    def lo_count(chunk, u, mine):
        return count(chunk, len(mine), len([v for v in mine if v <= u]))

    ctx = ExitStack()
    with ctx:
        def sb(name, shape, dt=F32):
            return ctx.enter_context(nc.sbuf_tensor(name, shape, dt))

        def ps(name, shape):
            return ctx.enter_context(nc.psum_tensor(name, shape, F32))

        def sem(name):
            return ctx.enter_context(nc.semaphore(name))

        scratch = nc.dram_tensor("gates_scratch", (NCHUNK, E, C), F32, kind="Internal").ap()

        ident = sb("ident", [P, P])
        ctxT = sb("ctxT", [P, NMAT, P])
        W1h, W1l = sb("W1h", [P, NE, H], F32R), sb("W1l", [P, NE, H], F32R)
        W2h, W2l = sb("W2h", [P, NE, D], F32R), sb("W2l", [P, NE, D], F32R)
        W2n = sb("W2n", [P, NE, D])
        rWh, rWl = sb("rWh", [P, NE], F32R), sb("rWl", [P, NE], F32R)
        rW = sb("rW", [P, NE])
        rb = sb("rb", [P, E])
        idx_raw, idx_neg, idx = sb("idx_raw", [1, S], I32), sb("idx_neg", [1, S], I32), sb("idx", [1, S], I32)
        gates_in, tg = sb("gates_in", [P, 2]), sb("tg", [P, 2])
        b1rows, b2rows, offrows = sb("b1rows", [NE, H]), sb("b2rows", [NE, D]), sb("offrows", [NE, D])
        b1T, nb1T, offT = sb("b1T", [P, NE]), sb("nb1T", [P, NE]), sb("offT", [P, NE])
        xin = [sb(f"xin{p}", [P, TI, D]) for p in range(2)]
        x1 = [sb(f"x1_{p}", [P, TI, D]) for p in range(2)]
        xn = sb("xn", [P, TI, D])
        xn2 = sb("xn2", [P, TI, D])
        xnT = sb("xnT", [P, TI, P])
        Wg = [sb(f"Wg{p}", [P, CS, P]) for p in range(2)]
        x2h = [sb(f"x2h{p}", [P, C], F32R) for p in range(2)]
        x2l = [sb(f"x2l{p}", [P, C], F32R) for p in range(2)]
        stats = sb("stats", [P, TI, 6])
        mv = sb("mv", [P, TI, 2])
        veps, rstd, mhalf = sb("veps", [P, TI]), sb("rstd", [P, TI]), sb("mhalf", [P, TI])
        lg = sb("lg", [P, TI, E])
        ex = sb("ex", [P, TI, E])
        mx, sm, rs = sb("mx", [P, TI]), sb("sm", [P, TI]), sb("rs", [P, TI])
        pr = sb("pr", [P, TI, EW])
        rest = sb("rest", [P, TI, EW])
        top = sb("top", [P, TI, 8])
        cw = sb("cw", [P, TI, NE])
        cwT = [sb(f"cwT{p}", [NE, C]) for p in range(2)]
        cwB = [sb(f"cwB{p}", [P, E, C]) for p in range(2)]
        t = [sb(f"t{n}", [P, C]) for n in range(NT)]
        th = [sb(f"th{n}", [P, C], F32R) for n in range(NT)]
        tl = [sb(f"tl{n}", [P, C], F32R) for n in range(NT)]
        ysb = sb("ysb", [P, C])
        ob = [sb(f"ob{p}", [P, TI, D]) for p in range(2)]
        early = cwB[1][:, :, :].rearrange("p e c -> p (e c)")
        ctxn = early[:, 0:NMAT * P].rearrange("p (m d) -> p m d", m=NMAT)
        W1n = early[:, NMAT * P:NMAT * P + NE * H].rearrange("p (e h) -> p e h", e=NE)

        z = [ps(f"z{n}", [P, C]) for n in range(NZ)]
        y = ps("y", [P, C])
        tp = ps("tp", [P, C])
        att = ps("att", [P, C])
        misc = ps("misc", [P, C])

        s_idx, s_gate, s_bias, s_w1, s_w2, s_rw = (sem(n) for n in
            ("idx_loaded", "g_loaded", "bias_loaded", "W1_loaded", "W2_loaded", "router_loaded"))
        s_ctx = [sem(f"ctx_loaded{n}") for n in range(2)]
        s_x = [sem(f"x_loaded{p}") for p in range(2)]
        s_wg = [sem(f"gathered{p}") for p in range(2)]
        s_scr = sem("gates_written")
        s_cwb = [[sem(f"gates_spread{p}_{g}") for g in range(CG)] for p in range(2)]
        s_out = [sem(f"out_stored{p}") for p in range(2)]
        s_ident, s_idv, s_idxok, s_rwpad, s_tg = (sem(n) for n in
            ("ident_made", "idx_step", "idx_ready", "router_padded", "tanh_ready"))
        s_ctp, s_ctev = sem("ctx_transposed"), sem("ctx_copied")
        s_b1T, s_b1c, s_off, s_offc, s_offT, s_offr = (sem(n) for n in
            ("b1_transposed", "b1_copied", "off_summed", "off_copied", "off_transposed", "off_ready"))
        s_whi, s_wlo, s_wrest = sem("W_hi_made"), sem("W_lo_made"), sem("rW_split")
        s_fill, s_mh = sem("fillers_set"), sem("minus_half_set")
        s_bn, s_ag, s_ve, s_rs1, s_xn = (sem(n) for n in
            ("ln1_stats", "ln1_meanvar", "ln1_var_eps", "ln1_rstd", "ln1_done"))
        s_bn2, s_ag2, s_ve2, s_rs2, s_xn2 = (sem(n) for n in
            ("ln2_stats", "ln2_meanvar", "ln2_var_eps", "ln2_rstd", "ln2_done"))
        s_t1, s_e1, s_att, s_x1, s_t2, s_x2h, s_x2l = (sem(n) for n in
            ("xn_transposed", "xnT_copied", "att_done", "x1_ready", "xn2_transposed", "x2_hi", "x2_lo"))
        s_lg, s_lb, s_mx, s_sub, s_exp, s_sm, s_rc, s_pr, s_top, s_low, s_mr, s_cw = (sem(n) for n in
            ("logits", "logits_biased", "logit_max", "logits_shifted", "exps", "exp_sum", "exp_sum_inv",
             "probs", "top8", "top3", "top_removed", "gates"))
        s_t3, s_cwT = sem("gates_transposed"), sem("gatesT_copied")
        s_z, s_a, s_hi, s_loP, s_loD, s_h2 = (sem(n) for n in
            ("z_done", "t_ready", "t_hi", "t_lo_pool", "t_lo_vector", "y_added"))
        s_y, s_ys, s_t4, s_fin = (sem(n) for n in ("y_done", "y_copied", "y_transposed", "out_ready"))

        block = ctx.enter_context(nc.Block())
        INNER = NCHUNK // 2 - 1

        @block.sync
        def _(sp):
            def load_x(c):
                k, r = c
                if r >= 2:
                    sp.wait_ge(s_x1, count(before(c, 2), 1, 1))
                for q in range(Q):
                    rows = x[:, bass.ds(k * (2 * CS) + (r * CS + TI * q), TI), :]
                    sp.dma_start(xin[r % 2][32 * q:32 * q + 32, :, :].rearrange("p i d -> p (i d)"),
                                 rows.rearrange("b i d -> b (i d)")).then_inc(s_x[r % 2], 16)

            def gather(c):
                k, r = c
                at = [sp.value_load(idx[0:1, bass.ds(k * (2 * CS) + (r * CS + n), 1)],
                                    min_val=0, max_val=NMAT - 1) for n in range(CS)]
                if r >= 2:
                    sp.wait_ge(s_att, count(before(c, 2), 1, 1))
                if r == 0:
                    sp.wait_ge(s_ctev, NMAT // TI)
                for n in range(CS):
                    sp.dma_start(Wg[r % 2][:, n, :],
                                 ctxT[:, bass.ds(at[n], 1), :].rearrange("p a o -> p (a o)"))\
                      .then_inc(s_wg[r % 2], 16)

            def spread_gates(c):
                k, r = c
                used = held(sp, f"used{r}", count(before(c, 1), NE)) if r >= 2 else 0
                written = held(sp, f"written{r}", count(c, 16, 16))
                sp.wait_ge(s_cwT, count(c, 1, 1))
                sp.dma_start(scratch[bass.ds(k * 2 + r, 1), :, :].rearrange("a e c -> (a e) c"),
                             cwT[r % 2][0:E, :]).then_inc(s_scr, 16)
                if r >= 2:
                    sp.wait_ge(s_a, used)
                elif r == 1:
                    sp.wait_ge(s_wlo, 4)
                    sp.wait_ge(s_ctp, NMAT // TI)
                sp.wait_ge(s_scr, written)
                for g, es in enumerate(GROUP):
                    src = scratch[bass.ds(k * 2 + r, 1), es[0]:es[-1] + 1, :].rearrange("a e c -> (a e c)")
                    sp.dma_start(cwB[r % 2][:, es[0]:es[-1] + 1, :].rearrange("p e c -> p (e c)"),
                                 src.partition_broadcast(P)).then_inc(s_cwb[r % 2][g], 16)

            def store(c):
                k, r = c
                sp.wait_ge(s_fin, count(c, 1, 1))
                for q in range(Q):
                    rows = out[:, bass.ds(k * (2 * CS) + (r * CS + TI * q), TI), :]
                    sp.dma_start(rows.rearrange("b i d -> b (i d)"),
                                 ob[r % 2][32 * q:32 * q + 32, :, :].rearrange("p i d -> p (i d)"))\
                      .then_inc(s_out[r % 2], 16)

            sp.dma_start(idx_raw[:, :], itok.rearrange("(a n) -> a n", a=1)).then_inc(s_idx, 16)
            load_x((0, 0))
            load_x((0, 1))
            half = NMAT // 2
            for n in range(2):
                sp.dma_start(ctxn[:, n * half:(n + 1) * half, :],
                             ctx_w[n * half:(n + 1) * half].rearrange("m o d -> o m d")).then_inc(s_ctx[n], 16)
            sp.dma_start(W1n[:, 0, :], sW1).then_inc(s_w1, 16)
            sp.dma_start(W1n[:, 1:NE, :], eW1.rearrange("e d h -> d e h")).then_inc(s_w1, 16)
            sp.dma_start(W2n[:, 0, :], sW2).then_inc(s_w2, 16)
            sp.dma_start(W2n[:, 1:NE, :], eW2.rearrange("e h d -> h e d")).then_inc(s_w2, 16)
            sp.wait_ge(s_idxok, 1)
            gather((0, 0))
            gather((0, 1))
            spread_gates((0, 0))
            load_x((0, 2))
            gather((0, 2))
            spread_gates((0, 1))
            with sp.Fori(0, INNER - 1) as k:
                for r in (1, 2):
                    store((k, r - 1))
                    load_x((k, r + 2))
                    gather((k, r + 2))
                    spread_gates((k, r + 1))
            store((INNER - 1, 0))
            load_x((INNER - 1, 3))
            gather((INNER - 1, 3))
            spread_gates((INNER - 1, 2))
            store((INNER - 1, 1))
            spread_gates((INNER - 1, 3))
            store((INNER, 0))
            store((INNER, 1))
            for p in range(2):
                sp.wait_ge(s_out[p], 16 * Q * (NCHUNK // 2))

        @block.gpsimd
        def _(pool):
            pool.memset(ident[:, :], 0.0).then_inc(s_ident, 1)
            pool.wait_ge(s_ident, 1)
            pool.affine_select(out=ident[:, :], in_=ident[:, :], compare_op=ALU.not_equal, fill=1.0,
                               base=0, pattern=[[-1, P]], channel_multiplier=1).then_inc(s_ident, 1)
            pool.memset(cw[:, :, E:NE], 1.0).then_inc(s_fill, 1)
            pool.memset(pr[:, :, E:EW], -1.0).then_inc(s_fill, 1)
            pool.memset(mhalf[:, :], -0.5).then_inc(s_mh, 1)
            pool.wait_ge(s_mh, 1)

            def rsqrt(c, ve, rsd):
                pool.wait_ge(ve, count(c, 1, 1))
                pool.tensor_tensor(rstd[:, :], veps[:, :], mhalf[:, :], ALU.pow).then_inc(rsd, 1)

            rsqrt((0, 0), s_ve, s_rs1)
            half = NE // 2
            for n, (raw, hi, lo) in enumerate(((W1n, W1h, W1l), (W2n, W2h, W2l))):
                for m in range(2):
                    pool.wait_ge(s_whi, 2 * n + m + 1)
                    sl = slice(m * half, (m + 1) * half)
                    pool.tensor_tensor(lo[:, sl, :], raw[:, sl, :], hi[:, sl, :].bitcast(F32),
                                       ALU.subtract).then_inc(s_wlo, 1)

            rsqrt((0, 0), s_ve2, s_rs2)

            def experts(c, front=True):
                for u in range(NE):
                    if front and u == 0:
                        rsqrt(after(c), s_ve, s_rs1)
                    if front and u == 4:
                        rsqrt(after(c), s_ve2, s_rs2)
                    if u not in POOL_LO:
                        continue
                    n = u % NT
                    pool.wait_ge(s_hi, count(c, NE, u + 1))
                    if c[1] > 0 or u >= NT:
                        pool.wait_ge(s_h2, count(c, NE, u + 1 - NT))
                    pool.tensor_tensor(tl[n][:, :], t[n][:, :], th[n][:, :].bitcast(F32),
                                       ALU.subtract).then_inc(s_loP, 1)

            experts((0, 0))
            with pool.Fori(0, INNER) as k:
                for r in (1, 2):
                    experts((k, r))
            experts((INNER, 1), False)

        @block.tensor
        def _(pe):
            def product(ps_out, wh, wl, xh, xl, start, stop, inc=None):
                nc.tensor.matmul(ps_out, wh, xh, start=start, stop=False)
                nc.tensor.matmul(ps_out, wh, xl, start=False, stop=False)
                return nc.tensor.matmul(ps_out, wl, xh, start=False, stop=stop)

            def transpose_xn(c):
                if c[1] > 0:
                    pe.wait_ge(s_cwT, count(c, 1))
                pe.wait_ge(s_xn, count(c, 1, 1))
                for i in range(TI):
                    mm = nc.tensor.transpose(tp[:, i * P:(i + 1) * P], xn[:, i, :], ident[:, :])
                mm.then_inc(s_t1, 1)

            def cross(c):
                pe.wait_ge(s_e1, count(c, 1, 1))
                pe.wait_ge(s_wg[c[1] % 2], count_slot(c, 16 * CS))
                if c[1] > 0:
                    pe.wait_ge(s_x1, count(c, 1))
                for i in range(TI):
                    for q in range(Q):
                        mm = nc.tensor.matmul(att[32 * q:32 * q + 32, i * D:(i + 1) * D],
                                              xnT[:, i, 32 * q:32 * q + 32], Wg[c[1] % 2][:, TI * q + i, :],
                                              start=True, stop=True)
                mm.then_inc(s_att, 1)

            def transpose_xn2(c):
                pe.wait_ge(s_xn2, count(c, 1, 1))
                for i in range(TI):
                    mm = nc.tensor.transpose(tp[:, i * P:(i + 1) * P], xn2[:, i, :], ident[:, :])
                mm.then_inc(s_t2, 1)

            def router(c):
                p = c[1] % 2
                pe.wait_ge(s_x2h, count(c, 1, 1))
                pe.wait_ge(s_x2l, count(c, 1, 1))
                if c[1] == 0:
                    pe.wait_ge(s_wrest, 2)
                if c[1] > 1:
                    pe.wait_ge(s_fin, count(before(c), 1))
                for i in range(TI):
                    sl = slice(i * P, (i + 1) * P)
                    mm = product(misc[:, i * NE:(i + 1) * NE], x2h[p][:, sl], x2l[p][:, sl],
                                 rWh[:, :], rWl[:, :], True, True)
                mm.then_inc(s_lg, 1)

            def transpose_gates(c):
                pe.wait_ge(s_cw, count(c, 1, 1))
                for i in range(TI):
                    mm = nc.tensor.transpose(tp[0:NE, i * P:(i + 1) * P], cw[:, i, :], ident[:, :])
                mm.then_inc(s_t3, 1)

            def first(c, u):
                p = c[1] % 2
                if u == 0:
                    pe.wait_ge(s_x2l, count(c, 1, 1))
                if c[1] > 0 or u >= NZ:
                    pe.wait_ge(s_a, count(c, NE, u + 1 - NZ))
                product(z[u % NZ][:, :], W1h[:, u, :], W1l[:, u, :], x2h[p][:, :], x2l[p][:, :],
                        True, True).then_inc(s_z, 1)

            def second(c, u):
                n = u % NT
                if u == 0 and c[1] > 0:
                    pe.wait_ge(s_ys, count(c, 1))
                pe.wait_ge(s_hi, count(c, NE, u + 1))
                if u in POOL_LO:
                    pe.wait_ge(s_loP, lo_count(c, u, POOL_LO))
                else:
                    pe.wait_ge(s_loD, lo_count(c, u, DVE_LO))
                product(y[:, :], W2h[:, u, :], W2l[:, u, :], th[n][:, :], tl[n][:, :],
                        u == 0, False).then_inc(s_h2, 1)

            def finish_y(c):
                nc.tensor.matmul(y[:, :], offrows[:, :], cwT[c[1] % 2][:, :], start=False, stop=True)\
                  .then_inc(s_y, 1)

            def transpose_y(c, logits_of):
                pe.wait_ge(s_ys, count(c, 1, 1))
                pe.wait_ge(s_lb, count(logits_of, 1, 1))
                for i in range(TI):
                    mm = nc.tensor.transpose(misc[:, i * P:(i + 1) * P], ysb[:, i * P:(i + 1) * P], ident[:, :])
                mm.then_inc(s_t4, 1)

            pe.wait_ge(s_ident, 2)
            transpose_xn((0, 0))
            for m in range(NMAT // TI):
                if m * TI % (NMAT // 2) == 0:
                    pe.wait_ge(s_ctx[m * TI // (NMAT // 2)], 16)
                if m >= NZ:
                    pe.wait_ge(s_ctev, m + 1 - NZ)
                for i in range(TI):
                    mm = nc.tensor.transpose(z[m % NZ][:, i * P:(i + 1) * P], ctxn[:, m * TI + i, :], ident[:, :])
                mm.then_inc(s_ctp, 1)
            pe.wait_ge(s_bias, 64)
            nc.tensor.transpose(misc[:, 0:NE], b1rows[:, :], ident[0:NE, 0:NE]).then_inc(s_b1T, 1)
            cross((0, 0))
            pe.wait_ge(s_b1c, 2)
            pe.wait_ge(s_w2, 32)
            for e in range(NE):
                mm = nc.tensor.matmul(misc[:, e:e + 1], W2n[:, (e + 1) % NE, :], b1T[:, e:e + 1], start=True, stop=True)
            mm.then_inc(s_off, 1)
            transpose_xn2((0, 0))
            pe.wait_ge(s_offc, 1)
            nc.tensor.transpose(misc[0:NE, P:2 * P], offT[:, :], ident[:, :]).then_inc(s_offT, 1)
            pe.wait_ge(s_offr, 1)
            router((0, 0))
            pe.wait_ge(s_ctev, NMAT // TI)
            pe.wait_ge(s_wlo, 4)

            def experts(c, front, prev=True):
                for u in range(NE):
                    first(c, u)
                    if u == 0 and not prev:
                        transpose_gates(c)
                    if u >= LAG:
                        second(c, u - LAG)
                    elif prev:
                        second(before(c), NE + u - LAG)
                    if u == LAG - 1 and prev:
                        finish_y(before(c))
                    if front:
                        if u == 1:
                            transpose_xn(after(c))
                        if u == 4:
                            cross(after(c))
                        if u == 7:
                            transpose_xn2(after(c))
                        if u == 8:
                            router(after(c))
                        if u == 11:
                            transpose_gates(after(c))
                    if u == LAG + 1 and prev:
                        transpose_y(before(c), c)

            experts((0, 0), True, prev=False)
            with pe.Fori(0, INNER) as k:
                for r in (1, 2):
                    experts((k, r), True)
            experts((INNER, 1), False)
            for u in range(NE - LAG, NE):
                second((INNER, 1), u)
            finish_y((INNER, 1))
            transpose_y((INNER, 1), (INNER, 1))

        @block.scalar
        def _(act):
            act.dma_start(gates_in[:, 0:1], g_xattn.partition_broadcast(P)).then_inc(s_gate, 16)
            act.dma_start(gates_in[:, 1:2], g_ffn.partition_broadcast(P)).then_inc(s_gate, 16)
            act.dma_start(b1rows[0:E, :], eb1).then_inc(s_bias, 16)
            act.dma_start(b1rows[E:NE, :], sb1.rearrange("(a n) -> a n", a=1)).then_inc(s_bias, 16)
            act.dma_start(b2rows[0:E, :], eb2).then_inc(s_bias, 16)
            act.dma_start(b2rows[E:NE, :], sb2.rearrange("(a n) -> a n", a=1)).then_inc(s_bias, 16)
            act.dma_start(rW[:, 0:E], router_W).then_inc(s_rw, 16)
            act.dma_start(rb[:, :], router_b.partition_broadcast(P)).then_inc(s_rw, 16)

            def copy_xnT(c):
                act.wait_ge(s_t1, count(c, 1, 1))
                if c[1] > 0:
                    act.wait_ge(s_att, count(c, 1))
                nc.scalar.activation(xnT[:, :, :].rearrange("p i t -> p (i t)"), tp[:, :], ACT.Copy).then_inc(s_e1, 1)

            def hi_x2(c):
                act.wait_ge(s_t2, count(c, 1, 1))
                if c[1] > 1:
                    act.wait_ge(s_z, count(before(c), NE))
                nc.scalar.activation(x2h[c[1] % 2][:, :], tp[:, :], ACT.Copy).then_inc(s_x2h, 1)

            def exps(c):
                act.wait_ge(s_sub, count(c, 1, 1))
                nc.scalar.activation(ex[:, :, :].rearrange("p i e -> p (i e)"),
                                     lg[:, :, :].rearrange("p i e -> p (i e)"), ACT.Exp).then_inc(s_exp, 1)

            def copy_gates(c):
                act.wait_ge(s_t3, count(c, 1, 1))
                if c[1] > 1:
                    act.wait_ge(s_y, count(before(c), 1))
                    act.wait_ge(s_scr, count(before(c), 16))
                nc.scalar.activation(cwT[c[1] % 2][:, :], tp[0:NE, :], ACT.Copy).then_inc(s_cwT, 1)

            def copy_y(c):
                act.wait_ge(s_y, count(c, 1, 1))
                if c[1] > 0:
                    act.wait_ge(s_t4, count(c, 1))
                nc.scalar.activation(ysb[:, :], y[:, :], ACT.Copy).then_inc(s_ys, 1)

            def experts(c, front, prev=True):
                for u in range(NE):
                    n = u % NT
                    act.wait_ge(s_a, count(c, NE, u + 1))
                    if c[1] > 0 or u >= NT:
                        act.wait_ge(s_h2, count(c, NE, u + 1 - NT))
                    nc.scalar.activation(th[n][:, :], t[n][:, :], ACT.Copy).then_inc(s_hi, 1)
                    if u == 0 and not prev:
                        copy_gates(c)
                    if front:
                        if u == 1:
                            copy_xnT(after(c))
                        if u == 6:
                            hi_x2(after(c))
                        if u == 8:
                            exps(after(c))
                        if u == 10:
                            copy_gates(after(c))
                    if u == LAG - 1 and prev:
                        copy_y(before(c))

            act.wait_ge(s_gate, 32)
            nc.scalar.activation(tg[:, :], gates_in[:, :], ACT.Tanh).then_inc(s_tg, 1)
            copy_xnT((0, 0))
            for m in range(0, NMAT // TI):
                act.wait_ge(s_ctp, m + 1)
                nc.scalar.activation(ctxT[:, m * TI:(m + 1) * TI, :].rearrange("p m o -> p (m o)"), z[m % NZ][:, :],
                                     ACT.Copy).then_inc(s_ctev, 1)
            half = NE // 2
            for n, (raw, hi, s) in enumerate(((W1n, W1h, s_w1), (W2n, W2h, s_w2))):
                act.wait_ge(s, 32)
                for m in range(2):
                    sl = slice(m * half, (m + 1) * half)
                    nc.scalar.activation(hi[:, sl, :].rearrange("p e h -> p (e h)"),
                                         raw[:, sl, :].rearrange("p e h -> p (e h)"), ACT.Copy).then_inc(s_whi, 1)
            hi_x2((0, 0))
            exps((0, 0))
            experts((0, 0), True, prev=False)
            with act.Fori(0, INNER) as k:
                for r in (1, 2):
                    experts((k, r), True)
            experts((INNER, 1), False)
            copy_y((INNER, 1))

        @block.vector
        def _(dve):
            def norm(c, turn, src, dst, bn, ag, ve, rsd, done):
                for i in range(TI):
                    last = nc.vector.bn_stats(stats[:, i, :], src[:, i, :])
                last.then_inc(bn, 1)
                dve.wait_ge(s_fill, 2)
                dve.wait_ge(bn, turn)
                for i in range(TI):
                    last = nc.vector.bn_aggr(mv[:, i, :], stats[:, i, :])
                last.then_inc(ag, 1)
                dve.wait_ge(ag, count(c, 1, 1))
                nc.vector.tensor_scalar_add(veps[:, :], mv[:, :, 1], EPS).then_inc(ve, 1)
                dve.wait_ge(rsd, count(c, 1, 1))
                for i in range(TI):
                    last = nc.vector.tensor_scalar(dst[:, i, :], src[:, i, :], mv[:, i, 0:1], rstd[:, i:i + 1],
                                                   ALU.subtract, ALU.mult)
                last.then_inc(done, 1)

            def norm1(c):
                turn = held(dve, f"norm1_{c[1]}", count(c, 1, 1))
                dve.wait_ge(s_x[c[1] % 2], count_slot(c, 16 * Q))
                if c[1] > 0:
                    dve.wait_ge(s_t1, count(c, 1))
                norm(c, turn, xin[c[1] % 2], xn, s_bn, s_ag, s_ve, s_rs1, s_xn)

            def add_cross(c):
                p = c[1] % 2
                if c[1] > 1:
                    dve.wait_ge(s_fin, count(before(c), 1))
                dve.wait_ge(s_att, count(c, 1, 1))
                nc.vector.scalar_tensor_tensor(x1[p][:, :, :].rearrange("p i d -> p (i d)"), att[:, :], tg[:, 0:1],
                                               xin[p][:, :, :].rearrange("p i d -> p (i d)"),
                                               ALU.mult, ALU.add).then_inc(s_x1, 1)

            def norm2(c):
                turn = held(dve, f"norm2_{c[1]}", count(c, 1, 1))
                dve.wait_ge(s_x1, count(c, 1, 1))
                if c[1] > 0:
                    dve.wait_ge(s_t2, count(c, 1))
                norm(c, turn, x1[c[1] % 2], xn2, s_bn2, s_ag2, s_ve2, s_rs2, s_xn2)

            def lo_x2(c):
                p = c[1] % 2
                dve.wait_ge(s_x2h, count(c, 1, 1))
                nc.vector.tensor_tensor(x2l[p][:, :], tp[:, :], x2h[p][:, :].bitcast(F32),
                                        ALU.subtract).then_inc(s_x2l, 1)

            def over_experts(a):
                return a[:, :].unsqueeze(2).to_broadcast([P, TI, E])

            def shift_logits(c):
                dve.wait_ge(s_lg, count(c, 1, 1))
                if c[1] > 0:
                    dve.wait_ge(s_exp, count(c, 1))
                nc.vector.tensor_tensor(lg[:, :, :], misc[:, 0:TI * NE].rearrange("p (i e) -> p i e", i=TI)[:, :, 0:E],
                                        rb[:, :].unsqueeze(1).to_broadcast([P, TI, E]), ALU.add).then_inc(s_lb, 1)
                dve.wait_ge(s_lb, count(c, 1, 1))
                nc.vector.reduce_max(mx[:, :], lg[:, :, :], AX.X).then_inc(s_mx, 1)
                dve.wait_ge(s_mx, count(c, 1, 1))
                nc.vector.tensor_tensor(lg[:, :, :], lg[:, :, :], over_experts(mx), ALU.subtract).then_inc(s_sub, 1)

            def choose(c):
                dve.wait_ge(s_exp, count(c, 1, 1))
                nc.vector.reduce_sum(sm[:, :], ex[:, :, :], AX.X).then_inc(s_sm, 1)
                dve.wait_ge(s_sm, count(c, 1, 1))
                nc.vector.reciprocal(rs[:, :], sm[:, :]).then_inc(s_rc, 1)
                dve.wait_ge(s_rc, count(c, 1, 1))
                nc.vector.tensor_tensor(pr[:, :, 0:E], ex[:, :, :], over_experts(rs), ALU.mult).then_inc(s_pr, 1)
                dve.wait_ge(s_fill, 2)
                dve.wait_ge(s_pr, count(c, 1, 1))
                for i in range(TI):
                    last = nc.vector.max(top[:, i, :], pr[:, i, 0:E])
                last.then_inc(s_top, 1)
                dve.wait_ge(s_top, count(c, 1, 1))
                nc.vector.memset(top[:, :, TOPK:8], -1.0).then_inc(s_low, 1)
                dve.wait_ge(s_fill, 2)
                dve.wait_ge(s_low, count(c, 1, 1))
                for i in range(TI):
                    last = nc.vector.match_replace(rest[:, i, :], top[:, i, :], pr[:, i, :], 0.0)
                last.then_inc(s_mr, 1)
                dve.wait_ge(s_mr, count(c, 1, 1))
                if c[1] > 0:
                    dve.wait_ge(s_t3, count(c, 1))
                nc.vector.tensor_tensor(cw[:, :, 0:E], pr[:, :, 0:E], rest[:, :, 0:E], ALU.subtract).then_inc(s_cw, 1)

            def add_y(c):
                k, r = c
                p = r % 2
                dve.wait_ge(s_t4, count(c, 1, 1))
                if r >= 2:
                    dve.wait_ge(s_out[p], count_slot(before(c, 2), 16 * Q))
                nc.vector.scalar_tensor_tensor(ob[p][:, :, :].rearrange("p i d -> p (i d)"), misc[:, :], tg[:, 1:2],
                                               x1[p][:, :, :].rearrange("p i d -> p (i d)"),
                                               ALU.mult, ALU.add).then_inc(s_fin, 1)

            def scale(c, u):
                n = u % NT
                k, r = c
                dve.wait_ge(s_z, count(c, NE, u + 1))
                if r > 0 or u >= NT:
                    v = (u - NT) % NE
                    of = c if u >= NT else before(c)
                    dve.wait_ge(s_hi, count(c, NE, u + 1 - NT))
                    if v in POOL_LO:
                        dve.wait_ge(s_loP, lo_count(of, v, POOL_LO))
                    else:
                        dve.wait_ge(s_loD, lo_count(of, v, DVE_LO))
                if u == 0:
                    nc.vector.tensor_scalar(t[n][:, :], z[u % NZ][:, :], nb1T[:, 0:1], None, ALU.max).then_inc(s_a, 1)
                    return
                for g, es in enumerate(GROUP):
                    if es[0] == u - 1:
                        dve.wait_ge(s_cwb[r % 2][g], count_slot(c, 16))
                nc.vector.scalar_tensor_tensor(t[n][:, :], z[u % NZ][:, :], nb1T[:, u:u + 1],
                                               cwB[r % 2][:, u - 1, :], ALU.max, ALU.mult).then_inc(s_a, 1)

            def low(c, u):
                n = u % NT
                dve.wait_ge(s_hi, count(c, NE, u + 1))
                if c[1] > 0 or u >= NT:
                    dve.wait_ge(s_h2, count(c, NE, u + 1 - NT))
                nc.vector.tensor_tensor(tl[n][:, :], t[n][:, :], th[n][:, :].bitcast(F32),
                                        ALU.subtract).then_inc(s_loD, 1)

            def experts(c, front, prev=True):
                for u in range(NE):
                    scale(c, u)
                    if u - 1 in DVE_LO:
                        low(c, u - 1)
                    if u == LAG + 2 and prev:
                        add_y(before(c))
                    if front:
                        if u == 0:
                            norm1(after(c))
                        if u == LAG + 2:
                            add_cross(after(c))
                            norm2(after(c))
                        if u == 6:
                            lo_x2(after(c))
                        if u == 8:
                            shift_logits(after(c))
                        if u == 9:
                            choose(after(c))
                if NE - 1 in DVE_LO:
                    low(c, NE - 1)

            dve.wait_ge(s_idx, 16)
            nc.vector.tensor_scalar(idx_neg[:, :], idx_raw[:, :], 0.0, float(NMAT), ALU.is_lt, ALU.mult).then_inc(s_idv, 1)
            dve.wait_ge(s_idv, 1)
            nc.vector.tensor_tensor(idx_raw[:, :], idx_raw[:, :], idx_neg[:, :], ALU.add).then_inc(s_idv, 1)
            dve.wait_ge(s_idv, 2)
            nc.vector.tensor_scalar(idx[:, :], idx_raw[:, :], 0.0, float(NMAT - 1), ALU.max, ALU.min).then_inc(s_idxok, 1)
            norm1((0, 0))
            nc.vector.memset(rW[:, E:NE], 0.0).then_inc(s_rwpad, 1)
            dve.wait_ge(s_rwpad, 1)
            dve.wait_ge(s_rw, 32)
            nc.vector.tensor_copy(rWh[:, :], rW[:, :]).then_inc(s_wrest, 1)
            dve.wait_ge(s_wrest, 1)
            nc.vector.tensor_tensor(rWl[:, :], rW[:, :], rWh[:, :].bitcast(F32), ALU.subtract).then_inc(s_wrest, 1)
            dve.wait_ge(s_b1T, 1)
            nc.vector.tensor_copy(b1T[:, :], misc[:, 0:NE]).then_inc(s_b1c, 1)
            nc.vector.tensor_scalar(nb1T[:, 0:1], misc[:, E:NE], -1.0, None, ALU.mult)
            nc.vector.tensor_scalar(nb1T[:, 1:NE], misc[:, 0:E], -1.0, None, ALU.mult).then_inc(s_b1c, 1)
            dve.wait_ge(s_tg, 1)
            add_cross((0, 0))
            norm2((0, 0))
            dve.wait_ge(s_off, 1)
            nc.vector.tensor_copy(offT[:, :], misc[:, 0:NE]).then_inc(s_offc, 1)
            dve.wait_ge(s_offT, 1)
            nc.vector.tensor_tensor(offrows[:, :], misc[0:NE, P:2 * P], b2rows[:, :], ALU.add).then_inc(s_offr, 1)
            lo_x2((0, 0))
            dve.wait_ge(s_fill, 2)
            shift_logits((0, 0))
            choose((0, 0))
            experts((0, 0), True, prev=False)
            with dve.Fori(0, INNER) as k:
                for r in (1, 2):
                    experts((k, r), True)
            experts((INNER, 1), False)
            add_y((INNER, 1))


_INS = ['x', 'itok_S_0_31', 'ctx_1024', 'g_xattn', 'g_ffn', 'L0_ffn_router_W', 'L0_ffn_router_b', 'L0_ffn_sW1',
        'L0_ffn_sb1', 'L0_ffn_sW2', 'L0_ffn_sb2', 'L0_ffn_eW1', 'L0_ffn_eb1', 'L0_ffn_eW2', 'L0_ffn_eb2']


def kernel(**inputs):
    import numpy as _np
    import concourse.bacc as _bacc
    from concourse import mybir as _mybir
    from concourse.bass_utils import run_bass_kernel_spmd as _run

    nc = _bacc.Bacc("TRN2", target_bir_lowering=False, num_devices=1)
    arrays, args = {}, []
    for name in _INS:
        a = _np.ascontiguousarray(inputs[name])
        arrays[f"in_{name}"] = a
        args.append(nc.dram_tensor(f"in_{name}", a.shape, _mybir.dt.from_np(a.dtype), kind="ExternalInput").ap())
    x = arrays["in_x"]
    out = nc.dram_tensor("out_dram", x.shape, _mybir.dt.from_np(x.dtype), kind="ExternalOutput").ap()
    gated_moe_block(nc, *args, out)
    r = _run(nc, [arrays], core_ids=[0])
    return r.results[0]["out_dram"]
```

```python
import numpy as np
import concourse.bass as bass
from concourse import mybir
from contextlib import ExitStack

F32 = mybir.dt.float32
F32R = mybir.dt.float32r
I32 = mybir.dt.int32
ALU = mybir.AluOpType
ACT = mybir.ActivationFunctionType
AX = mybir.AxisListType

EPS = 1e-5
TOPK = 3


def count(chunk, per, plus=0):
    k, r = chunk
    return k * (2 * per) + (r * per + plus)


def count_slot(chunk, per):
    k, r = chunk
    return k * per + ((r // 2 + 1) * per)


def held(eng, name, value):
    if isinstance(value, int):
        return value
    reg = eng.alloc_register(name)
    eng.reg_mov(reg, value)
    return reg


def before(chunk, n=1):
    return (chunk[0], chunk[1] - n)


def after(chunk):
    return (chunk[0], chunk[1] + 1)


def gated_moe_block(nc, x, itok, ctx_w, g_xattn, g_ffn, router_W, router_b, sW1, sb1, sW2, sb2,
                    eW1, eb1, eW2, eb2, out):
    NB, S, D = x.shape
    NMAT = ctx_w.shape[0]
    E = router_W.shape[1]
    NE = E + 1
    Q = 4
    TI = 4
    CS = Q * TI
    C = CS * NB
    NCHUNK = S // CS
    P = 128
    H = sW1.shape[1]
    assert D == P and H == P and NB == 32 and NCHUNK % 2 == 0
    NZ = 4
    NT = 4
    LAG = 3
    A_USUAL = dict(N1=3, T1=6, XT=6, CR=8, AX=9, S2=10, RS=11, NM=12, N2=12)
    B_USUAL = dict(T2=1, H2=1, LO=1, RT=2, SH=3, EX=3, CH=4, T3=6, CG=6)
    A_ONE = dict(CR=1, AX=2, S2=3, RS=4, NM=5, N2=5)
    B_ONE = dict(T2=7, H2=7, LO=7, RT=8, SH=9, EX=9, CH=9, T3=11, CG=11)
    A_TWO = dict(N1=7, T1=12, XT=12, CR=13, AX=13, S2=13, RS=14, NM=15, N2=14)
    TY, YC, AY = 4, 2, 5

    def plan(c, last=NCHUNK):
        one, two = after(c), after(after(c))
        if c[1] == 0:
            return [(one, A_ONE), (one, B_ONE), (two, A_TWO)]
        return [(one, B_USUAL)] * (last > 1) + [(two, A_USUAL)] * (last > 2)

    CG = 4
    GROUP = [range(0, 3), range(3, 7), range(7, 11), range(11, 15)]
    PADK = TOPK + 5
    EW = E + 5

    DVE_LO = [1, 6, 10, 15]
    POOL_LO = [u for u in range(NE) if u not in DVE_LO]

    def lo_count(chunk, u, mine):
        return count(chunk, len(mine), len([v for v in mine if v <= u]))

    ctx = ExitStack()
    with ctx:
        def sb(name, shape, dt=F32):
            return ctx.enter_context(nc.sbuf_tensor(name, shape, dt))

        def ps(name, shape):
            return ctx.enter_context(nc.psum_tensor(name, shape, F32))

        def sem(name):
            return ctx.enter_context(nc.semaphore(name))

        scratch = nc.dram_tensor("gates_scratch", (NCHUNK, E, C), F32, kind="Internal").ap()

        ident = sb("ident", [P, P])
        ctxT = sb("ctxT", [P, NMAT, P])
        W1h, W1l = sb("W1h", [P, NE, H], F32R), sb("W1l", [P, NE, H], F32R)
        W2h, W2l = sb("W2h", [P, NE, D], F32R), sb("W2l", [P, NE, D], F32R)
        W2n = sb("W2n", [P, NE, D])
        rWh, rWl = sb("rWh", [P, NE], F32R), sb("rWl", [P, NE], F32R)
        rW = sb("rW", [P, NE])
        rb = sb("rb", [P, E])
        idx_raw, idx_neg, idx = sb("idx_raw", [1, S], I32), sb("idx_neg", [1, S], I32), sb("idx", [1, S], I32)
        gates_in, tg = sb("gates_in", [P, 2]), sb("tg", [P, 2])
        b1rows, b2rows, offrows = sb("b1rows", [NE, H]), sb("b2rows", [NE, D]), sb("offrows", [NE, D])
        b1T, nb1T, offT = sb("b1T", [P, NE]), sb("nb1T", [P, NE]), sb("offT", [P, NE])
        NTILE = NCHUNK * TI
        xs = sb("xs", [P, NTILE, D])
        xn = sb("xn", [P, TI, D])
        xn2 = sb("xn2", [P, TI, D])
        xnT = sb("xnT", [P, TI, P])
        Wg = [sb(f"Wg{p}", [P, CS, P]) for p in range(2)]
        x2h = [sb(f"x2h{p}", [P, C], F32R) for p in range(2)]
        x2l = [sb(f"x2l{p}", [P, C], F32R) for p in range(2)]
        stats1, mv1 = sb("stats1", [P, NTILE, 6]), sb("mv1", [P, NTILE, 2])
        veps1, rstd1, nmr1 = sb("veps1", [P, NTILE]), sb("rstd1", [P, NTILE]), sb("nmr1", [P, NTILE])
        stats2, mv2 = sb("stats2", [P, TI, 6]), sb("mv2", [P, TI, 2])
        veps2, rstd2, nmr2 = sb("veps2", [P, TI]), sb("rstd2", [P, TI]), sb("nmr2", [P, TI])
        mhalf = sb("mhalf", [P, NTILE])
        lg = sb("lg", [P, TI, E])
        ex = sb("ex", [P, TI, E])
        mx, sm, rs = sb("mx", [P, TI]), sb("sm", [P, TI]), sb("rs", [P, TI])
        pr = sb("pr", [P, TI, EW])
        rest = sb("rest", [P, TI, EW])
        top = sb("top", [P, TI, 8])
        cw = sb("cw", [P, TI, NE])
        cwT = [sb(f"cwT{p}", [NE, C]) for p in range(2)]
        cwB = [sb(f"cwB{p}", [P, E, C]) for p in range(2)]
        t = [sb(f"t{n}", [P, C]) for n in range(NT)]
        th = [sb(f"th{n}", [P, C], F32R) for n in range(NT)]
        tl = [sb(f"tl{n}", [P, C], F32R) for n in range(NT)]
        ysb = sb("ysb", [P, C])
        ob = [sb(f"ob{p}", [P, TI, D]) for p in range(2)]
        early = cwB[1][:, :, :].rearrange("p e c -> p (e c)")
        ctxn = early[:, 0:NMAT * P].rearrange("p (m d) -> p m d", m=NMAT)
        ctx0 = cwB[0][:, :, :].rearrange("p e c -> p (e c)")[:, 0:CS * P].rearrange("p (n d) -> p n d", n=CS)
        W1n = early[:, NMAT * P:NMAT * P + NE * H].rearrange("p (e h) -> p e h", e=NE)

        z = [ps(f"z{n}", [P, C]) for n in range(NZ)]
        y = ps("y", [P, C])
        tp = ps("tp", [P, C])
        att = ps("att", [P, C])
        misc = ps("misc", [P, C])

        s_idx, s_gate, s_bias, s_w1, s_w2, s_rw = (sem(n) for n in
            ("idx_loaded", "g_loaded", "bias_loaded", "W1_loaded", "W2_loaded", "router_loaded"))
        s_ctx = [sem(f"ctx_loaded{n}") for n in range(2)]
        s_x = [sem("x_first_loaded"), sem("x_rest_loaded")]
        s_c0 = [sem(f"ctx_first_loaded{i}") for i in range(TI)]
        s_wg = [sem(f"gathered{p}") for p in range(2)]
        s_scr = sem("gates_written")
        s_cwb = [[sem(f"gates_spread{p}_{g}") for g in range(CG)] for p in range(2)]
        s_out = [sem(f"out_stored{p}") for p in range(2)]
        s_ident, s_idv, s_idxok, s_rwpad, s_tg = (sem(n) for n in
            ("ident_made", "idx_step", "idx_ready", "router_padded", "tanh_ready"))
        s_ctp, s_ctA, s_ctD = sem("ctx_transposed"), sem("ctx_copied_scalar"), sem("ctx_copied_vector")
        s_b1T, s_b1c, s_off, s_offc, s_offT, s_offr = (sem(n) for n in
            ("b1_transposed", "b1_copied", "off_summed", "off_copied", "off_transposed", "off_ready"))
        s_whi, s_wlo, s_w2lo, s_wrest = (sem(n) for n in ("W_hi_made", "W1_lo_made", "W2_lo_made", "rW_split"))
        s_fill, s_mh = sem("fillers_set"), sem("minus_half_set")
        s_bn, s_ag, s_ve, s_rs1, s_nm1, s_xn = (sem(n) for n in
            ("ln1_stats", "ln1_meanvar", "ln1_var_eps", "ln1_rstd", "ln1_shift", "ln1_done"))
        s_bn2, s_ag2, s_ve2, s_rs2, s_nm2, s_xn2 = (sem(n) for n in
            ("ln2_stats", "ln2_meanvar", "ln2_var_eps", "ln2_rstd", "ln2_shift", "ln2_done"))
        s_c0t, s_c0c = sem("ctx_first_transposed"), sem("ctx_first_copied")
        s_t1, s_e1, s_att, s_x1, s_t2, s_x2h, s_x2l = (sem(n) for n in
            ("xn_transposed", "xnT_copied", "att_done", "x1_ready", "xn2_transposed", "x2_hi", "x2_lo"))
        s_lg, s_lb, s_mx, s_sub, s_exp, s_sm, s_rc, s_pr, s_top, s_low, s_mr, s_cw = (sem(n) for n in
            ("logits", "logits_biased", "logit_max", "logits_shifted", "exps", "exp_sum", "exp_sum_inv",
             "probs", "top8", "top3", "top_removed", "gates"))
        s_t3, s_cwT = sem("gates_transposed"), sem("gatesT_copied")
        s_z, s_a, s_hi, s_loP, s_loD, s_h2 = (sem(n) for n in
            ("z_done", "t_ready", "t_hi", "t_lo_pool", "t_lo_vector", "y_added"))
        s_y, s_ys, s_t4, s_fin = (sem(n) for n in ("y_done", "y_copied", "y_transposed", "out_ready"))

        block = ctx.enter_context(nc.Block())
        LOOPS = (NCHUNK - 4) // 2
        TAIL = [(LOOPS, 1), (LOOPS, 2), (LOOPS, 3)]

        @block.sync
        def _(sp):
            def load_x(c0, c1, loaded):
                for q in range(Q):
                    rows = x.rearrange("b (c q i) d -> q b c (i d)", q=Q, i=TI)[q, :, c0:c1, :]
                    sp.dma_start(xs[32 * q:32 * q + 32, c0 * TI:c1 * TI, :].rearrange("p (c i) d -> p c (i d)", i=TI),
                                 rows).then_inc(loaded, 16)

            def matrices_of(c):
                k, r = c
                return nc.values_load_multi_w_load_instructions(
                    idx[0:1, bass.ds(k * (2 * CS) + r * CS, CS)], engines=(sp.engine,), min_val=0, max_val=NMAT - 1,
                    skip_runtime_bounds_check_because="brought into range on the chip")[1]

            def gather(c, at):
                k, r = c
                if r >= 2:
                    sp.wait_ge(s_att, count(before(c, 2), 1, 1))
                if r == 1:
                    sp.wait_ge(s_ctA, NMAT // TI // 2)
                    sp.wait_ge(s_ctD, NMAT // TI // 2)
                for n in range(CS):
                    sp.dma_start(Wg[r % 2][:, n, :],
                                 ctxT[:, bass.ds(at[n], 1), :].rearrange("p a o -> p (a o)"))\
                      .then_inc(s_wg[r % 2], 16)

            def spread_gates(c):
                k, r = c
                used = held(sp, f"used{r}", count(before(c, 1), NE)) if r >= 2 else 0
                written = held(sp, f"written{r}", count(c, 16, 16))
                sp.wait_ge(s_cwT, count(c, 1, 1))
                sp.dma_start(scratch[bass.ds(k * 2 + r, 1), :, :].rearrange("a e c -> (a e) c"),
                             cwT[r % 2][0:E, :]).then_inc(s_scr, 16)
                if r >= 2:
                    sp.wait_ge(s_a, used)
                elif r == 1:
                    sp.wait_ge(s_wlo, 2)
                    sp.wait_ge(s_ctp, NMAT // TI)
                else:
                    sp.wait_ge(s_c0t, TI)
                sp.wait_ge(s_scr, written)
                for g, es in enumerate(GROUP):
                    src = scratch[bass.ds(k * 2 + r, 1), es[0]:es[-1] + 1, :].rearrange("a e c -> (a e c)")
                    sp.dma_start(cwB[r % 2][:, es[0]:es[-1] + 1, :].rearrange("p e c -> p (e c)"),
                                 src.partition_broadcast(P)).then_inc(s_cwb[r % 2][g], 16)

            def store(c):
                k, r = c
                sp.wait_ge(s_fin, count(c, 1, 1))
                for q in range(Q):
                    rows = out[:, bass.ds(k * (2 * CS) + (r * CS + TI * q), TI), :]
                    sp.dma_start(rows.rearrange("b i d -> b (i d)"),
                                 ob[r % 2][32 * q:32 * q + 32, :, :].rearrange("p i d -> p (i d)"))\
                      .then_inc(s_out[r % 2], 16)

            sp.dma_start(idx_raw[:, :], itok.rearrange("(a n) -> a n", a=1)).then_inc(s_idx, 16)
            load_x(0, 1, s_x[0])
            sp.wait_ge(s_idxok, 1)
            at = matrices_of((0, 0))
            for i in range(TI):
                for q in range(Q):
                    sp.dma_start(ctx0[:, i * Q + q, :],
                                 ctx_w[bass.ds(at[TI * q + i], 1), :, :].rearrange("a o d -> (a o) d"))\
                      .then_inc(s_c0[i], 16)
            half = NMAT // 2
            for n in range(2):
                sp.dma_start(ctxn[:, n * half:(n + 1) * half, :],
                             ctx_w[n * half:(n + 1) * half].rearrange("m o d -> o m d")).then_inc(s_ctx[n], 16)
            sp.dma_start(W1n[:, 0, :], sW1).then_inc(s_w1, 16)
            sp.dma_start(W1n[:, 1:NE, :], eW1.rearrange("e d h -> d e h")).then_inc(s_w1, 16)
            load_x(1, NCHUNK, s_x[1])
            sp.dma_start(W2n[:, 0, :], sW2).then_inc(s_w2, 16)
            sp.dma_start(W2n[:, 1:NE, :], eW2.rearrange("e h d -> h e d")).then_inc(s_w2, 16)
            at = matrices_of((0, 1))
            spread_gates((0, 0))
            gather((0, 1), at)
            gather((0, 2), matrices_of((0, 2)))
            at = matrices_of((0, 3))
            spread_gates((0, 1))
            gather((0, 3), at)
            with sp.Fori(0, LOOPS) as k:
                for r in (1, 2):
                    at = matrices_of((k, r + 3))
                    store((k, r - 1))
                    spread_gates((k, r + 1))
                    gather((k, r + 3), at)
            for c in TAIL[:-1]:
                store(before(c))
                spread_gates(after(c))
            store(before(TAIL[-1]))
            store(TAIL[-1])
            for p in range(2):
                sp.wait_ge(s_out[p], 16 * Q * (NCHUNK // 2))

        @block.gpsimd
        def _(pool):
            pool.memset(ident[:, :], 0.0).then_inc(s_ident, 1)
            pool.wait_ge(s_ident, 1)
            pool.affine_select(out=ident[:, :], in_=ident[:, :], compare_op=ALU.not_equal, fill=1.0,
                               base=0, pattern=[[-1, P]], channel_multiplier=1).then_inc(s_ident, 1)
            pool.memset(cw[:, :, E:NE], 1.0).then_inc(s_fill, 1)
            pool.memset(pr[:, :, E:EW], -1.0).then_inc(s_fill, 1)
            pool.memset(mhalf[:, :], -0.5).then_inc(s_mh, 1)
            pool.wait_ge(s_mh, 1)

            def rsqrt(veps, rstd, ve, rsd, turn):
                pool.wait_ge(ve, turn)
                pool.tensor_tensor(rstd, veps, mhalf[:, 0:veps.shape[-1]], ALU.pow).then_inc(rsd, 1)

            rsqrt(veps1[:, 0:TI], rstd1[:, 0:TI], s_ve, s_rs1, 1)
            rsqrt(veps2[:, :], rstd2[:, :], s_ve2, s_rs2, 1)
            rsqrt(veps1[:, TI:NTILE], rstd1[:, TI:NTILE], s_ve, s_rs1, 2)
            half = NE // 2
            for m in range(2):
                pool.wait_ge(s_whi, m + 3)
                sl = slice(m * half, (m + 1) * half)
                pool.tensor_tensor(W2l[:, sl, :], W2n[:, sl, :], W2h[:, sl, :].bitcast(F32),
                                   ALU.subtract).then_inc(s_w2lo, 1)


            def experts(c, todo):
                for u in range(NE):
                    for f, at in todo:
                        if at.get("RS") == u:
                            rsqrt(veps2[:, :], rstd2[:, :], s_ve2, s_rs2, count(f, 1, 1))
                    if u not in POOL_LO:
                        continue
                    n = u % NT
                    pool.wait_ge(s_hi, count(c, NE, u + 1))
                    if c[1] > 0 or u >= NT:
                        pool.wait_ge(s_h2, count(c, NE, u + 1 - NT))
                    pool.tensor_tensor(tl[n][:, :], t[n][:, :], th[n][:, :].bitcast(F32),
                                       ALU.subtract).then_inc(s_loP, 1)

            experts((0, 0), plan((0, 0)))
            with pool.Fori(0, LOOPS) as k:
                for r in (1, 2):
                    experts((k, r), plan((k, r)))
            for n, c in enumerate(TAIL):
                experts(c, plan(c, len(TAIL) - n))

        @block.tensor
        def _(pe):
            def product(ps_out, wh, wl, xh, xl, start, stop, inc=None):
                nc.tensor.matmul(ps_out, wh, xh, start=start, stop=False)
                nc.tensor.matmul(ps_out, wh, xl, start=False, stop=False)
                return nc.tensor.matmul(ps_out, wl, xh, start=False, stop=stop)

            def transpose_xn(c):
                if c[1] > 0:
                    pe.wait_ge(s_cwT, count(c, 1))
                pe.wait_ge(s_xn, count(c, 2, 2))
                for i in range(TI):
                    mm = nc.tensor.transpose(tp[:, i * P:(i + 1) * P], xn[:, i, :], ident[:, :])
                mm.then_inc(s_t1, 1)

            def cross(c):
                pe.wait_ge(s_e1, count(c, 1, 1))
                if c[1] == 0:
                    pe.wait_ge(s_c0c, TI)
                elif c[1] % 2:
                    pe.wait_ge(s_wg[1], count_slot(c, 16 * CS))
                else:
                    pe.wait_ge(s_wg[0], count_slot(before(c, 2), 16 * CS))
                if c[1] > 0:
                    pe.wait_ge(s_x1, count(c, 1))
                for i in range(TI):
                    for q in range(Q):
                        mm = nc.tensor.matmul(att[32 * q:32 * q + 32, i * D:(i + 1) * D],
                                              xnT[:, i, 32 * q:32 * q + 32], Wg[c[1] % 2][:, TI * q + i, :],
                                              start=True, stop=True)
                mm.then_inc(s_att, 1)

            def transpose_xn2(c):
                pe.wait_ge(s_xn2, count(c, 2, 2))
                for i in range(TI):
                    mm = nc.tensor.transpose(tp[:, i * P:(i + 1) * P], xn2[:, i, :], ident[:, :])
                mm.then_inc(s_t2, 1)

            def router(c):
                p = c[1] % 2
                pe.wait_ge(s_x2h, count(c, 1, 1))
                pe.wait_ge(s_x2l, count(c, 1, 1))
                if c[1] == 0:
                    pe.wait_ge(s_wrest, 2)
                if c[1] > 2:
                    pe.wait_ge(s_fin, count(before(c, 2), 1))
                for i in range(TI):
                    sl = slice(i * P, (i + 1) * P)
                    mm = product(misc[:, i * NE:(i + 1) * NE], x2h[p][:, sl], x2l[p][:, sl],
                                 rWh[:, :], rWl[:, :], True, True)
                mm.then_inc(s_lg, 1)

            def transpose_gates(c):
                pe.wait_ge(s_cw, count(c, 1, 1))
                for i in range(TI):
                    mm = nc.tensor.transpose(tp[0:NE, i * P:(i + 1) * P], cw[:, i, :], ident[:, :])
                mm.then_inc(s_t3, 1)

            def first(c, u):
                p = c[1] % 2
                if u == 0:
                    pe.wait_ge(s_x2l, count(c, 1, 1))
                if c[1] > 0 or u >= NZ:
                    pe.wait_ge(s_a, count(c, NE, u + 1 - NZ))
                product(z[u % NZ][:, :], W1h[:, u, :], W1l[:, u, :], x2h[p][:, :], x2l[p][:, :],
                        True, True).then_inc(s_z, 1)

            def second(c, u):
                n = u % NT
                if u == 0 and c[1] > 0:
                    pe.wait_ge(s_ys, count(c, 1))
                pe.wait_ge(s_hi, count(c, NE, u + 1))
                if u in POOL_LO:
                    pe.wait_ge(s_loP, lo_count(c, u, POOL_LO))
                else:
                    pe.wait_ge(s_loD, lo_count(c, u, DVE_LO))
                product(y[:, :], W2h[:, u, :], W2l[:, u, :], th[n][:, :], tl[n][:, :],
                        u == 0, False).then_inc(s_h2, 1)

            def finish_y(c):
                nc.tensor.matmul(y[:, :], offrows[:, :], cwT[c[1] % 2][:, :], start=False, stop=True)\
                  .then_inc(s_y, 1)

            def transpose_y(c, logits_of):
                pe.wait_ge(s_ys, count(c, 1, 1))
                pe.wait_ge(s_lb, count(logits_of, 1, 1))
                for i in range(TI):
                    mm = nc.tensor.transpose(misc[:, i * P:(i + 1) * P], ysb[:, i * P:(i + 1) * P], ident[:, :])
                mm.then_inc(s_t4, 1)

            pe.wait_ge(s_ident, 2)
            transpose_xn((0, 0))
            for i in range(TI):
                pe.wait_ge(s_c0[i], 16 * Q)
                for q in range(Q):
                    mm = nc.tensor.transpose(z[i][:, q * P:(q + 1) * P], ctx0[:, i * Q + q, :], ident[:, :])
                mm.then_inc(s_c0t, 1)
            pe.wait_ge(s_bias, 64)
            nc.tensor.transpose(misc[:, 0:NE], b1rows[:, :], ident[0:NE, 0:NE]).then_inc(s_b1T, 1)
            cross((0, 0))

            def transpose_ctx(m):
                if m * TI % (NMAT // 2) == 0:
                    pe.wait_ge(s_ctx[m * TI // (NMAT // 2)], 16)
                if m < NZ:
                    pe.wait_ge(s_c0c, m + 1)
                else:
                    pe.wait_ge(s_ctD if m % 2 else s_ctA, (m - NZ) // 2 + 1)
                for i in range(TI):
                    mm = nc.tensor.transpose(z[m % NZ][:, i * P:(i + 1) * P], ctxn[:, m * TI + i, :], ident[:, :])
                mm.then_inc(s_ctp, 1)

            transpose_xn2((0, 0))
            pe.wait_ge(s_b1c, 2)
            router((0, 0))
            for m in range(NZ):
                transpose_ctx(m)
            transpose_gates((0, 0))
            for m in range(NZ, NMAT // TI):
                transpose_ctx(m)
            pe.wait_ge(s_w2, 32)
            for e in range(NE):
                mm = nc.tensor.matmul(misc[:, e:e + 1], W2n[:, (e + 1) % NE, :], b1T[:, e:e + 1], start=True, stop=True)
            mm.then_inc(s_off, 1)
            transpose_xn((0, 1))
            pe.wait_ge(s_ctA, NMAT // TI // 2)
            pe.wait_ge(s_ctD, NMAT // TI // 2)
            pe.wait_ge(s_wlo, 2)

            def experts(c, todo, left=NCHUNK):
                for u in range(NE):
                    first(c, u)
                    if u == LAG - 1 and c[1] == 0:
                        pe.wait_ge(s_offc, 1)
                        nc.tensor.transpose(misc[0:NE, P:2 * P], offT[:, :], ident[:, :]).then_inc(s_offT, 1)
                        pe.wait_ge(s_offr, 1)
                        pe.wait_ge(s_w2lo, 2)
                    if u >= LAG:
                        second(c, u - LAG)
                    elif c[1] > 0:
                        second(before(c), NE + u - LAG)
                    if u == LAG - 1 and c[1] > 0:
                        finish_y(before(c))
                    for f, at in todo:
                        if at.get("T1") == u:
                            transpose_xn(f)
                        if at.get("CR") == u:
                            cross(f)
                        if at.get("T2") == u:
                            transpose_xn2(f)
                        if at.get("RT") == u:
                            router(f)
                        if at.get("T3") == u:
                            transpose_gates(f)
                    if u == TY and c[1] > 0:
                        transpose_y(before(c), after(c) if left > 1 else c)

            experts((0, 0), plan((0, 0)))
            with pe.Fori(0, LOOPS) as k:
                for r in (1, 2):
                    experts((k, r), plan((k, r)))
            for n, c in enumerate(TAIL):
                experts(c, plan(c, len(TAIL) - n), len(TAIL) - n)
            for u in range(NE - LAG, NE):
                second(c, u)
            finish_y(c)
            transpose_y(c, c)

        @block.scalar
        def _(act):
            act.dma_start(gates_in[:, 0:1], g_xattn.partition_broadcast(P)).then_inc(s_gate, 16)
            act.dma_start(gates_in[:, 1:2], g_ffn.partition_broadcast(P)).then_inc(s_gate, 16)
            act.dma_start(b1rows[0:E, :], eb1).then_inc(s_bias, 16)
            act.dma_start(b1rows[E:NE, :], sb1.rearrange("(a n) -> a n", a=1)).then_inc(s_bias, 16)
            act.dma_start(b2rows[0:E, :], eb2).then_inc(s_bias, 16)
            act.dma_start(b2rows[E:NE, :], sb2.rearrange("(a n) -> a n", a=1)).then_inc(s_bias, 16)
            act.dma_start(rW[:, 0:E], router_W).then_inc(s_rw, 16)
            act.dma_start(rb[:, :], router_b.partition_broadcast(P)).then_inc(s_rw, 16)

            def norm(c, i0, dst, rstd, nmr, done, dyn):
                k, r = c
                for i in (i0, i0 + 1):
                    at = bass.ds(k * (2 * TI) + (r * TI + i), 1)
                    own = at if dyn else slice(i, i + 1)
                    last = nc.scalar.activation(dst[:, i, :], xs[:, at, :].rearrange("p a d -> p (a d)"),
                                                ACT.Identity, bias=nmr[:, own], scale=rstd[:, own])
                last.then_inc(done, 1)

            def norm1(c, i0):
                norm(c, i0, xn, rstd1, nmr1, s_xn, True)

            def norm2(c, i0):
                norm(c, i0, xn2, rstd2, nmr2, s_xn2, False)

            def copy_xnT(c):
                act.wait_ge(s_t1, count(c, 1, 1))
                if c[1] > 0:
                    act.wait_ge(s_att, count(c, 1))
                nc.scalar.activation(xnT[:, :, :].rearrange("p i t -> p (i t)"), tp[:, :], ACT.Copy).then_inc(s_e1, 1)

            def hi_x2(c):
                act.wait_ge(s_t2, count(c, 1, 1))
                if c[1] > 1:
                    act.wait_ge(s_z, count(before(c), NE))
                nc.scalar.activation(x2h[c[1] % 2][:, :], tp[:, :], ACT.Copy).then_inc(s_x2h, 1)

            def exps(c):
                act.wait_ge(s_sub, count(c, 1, 1))
                nc.scalar.activation(ex[:, :, :].rearrange("p i e -> p (i e)"),
                                     lg[:, :, :].rearrange("p i e -> p (i e)"), ACT.Exp).then_inc(s_exp, 1)

            def copy_gates(c):
                act.wait_ge(s_t3, count(c, 1, 1))
                if c[1] > 1:
                    act.wait_ge(s_y, count(before(c), 1))
                    act.wait_ge(s_scr, count(before(c), 16))
                nc.scalar.activation(cwT[c[1] % 2][:, :], tp[0:NE, :], ACT.Copy).then_inc(s_cwT, 1)

            def copy_y(c):
                act.wait_ge(s_y, count(c, 1, 1))
                if c[1] > 0:
                    act.wait_ge(s_t4, count(c, 1))
                nc.scalar.activation(ysb[:, :], y[:, :], ACT.Copy).then_inc(s_ys, 1)

            def experts(c, todo):
                for u in range(NE):
                    n = u % NT
                    for f, at in todo:
                        if at.get("N1") == u:
                            act.wait_ge(s_t1, count(f, 1))
                        if at.get("N2") == u:
                            act.wait_ge(s_nm2, count(f, 1, 1))
                            act.wait_ge(s_t2, count(f, 1))
                    act.wait_ge(s_a, count(c, NE, u + 1))
                    if c[1] > 0 or u >= NT:
                        act.wait_ge(s_h2, count(c, NE, u + 1 - NT))
                    nc.scalar.activation(th[n][:, :], t[n][:, :], ACT.Copy).then_inc(s_hi, 1)
                    for f, at in todo:
                        for half in range(2):
                            if at.get("N1") == u - half:
                                norm1(f, 2 * half)
                            if at.get("N2") == u - half:
                                norm2(f, 2 * half)
                        if at.get("XT") == u:
                            copy_xnT(f)
                        if at.get("H2") == u:
                            hi_x2(f)
                        if at.get("EX") == u:
                            exps(f)
                        if at.get("CG") == u:
                            copy_gates(f)
                    if u == YC and c[1] > 0:
                        copy_y(before(c))

            act.wait_ge(s_gate, 32)
            nc.scalar.activation(tg[:, :], gates_in[:, :], ACT.Tanh).then_inc(s_tg, 1)
            act.wait_ge(s_nm1, 1)
            norm1((0, 0), 0)
            norm1((0, 0), 2)
            copy_xnT((0, 0))
            for i in range(TI):
                act.wait_ge(s_c0t, i + 1)
                nc.scalar.activation(Wg[0][:, i:CS:TI, :], z[i][:, :].rearrange("p (q o) -> p q o", q=Q),
                                     ACT.Copy).then_inc(s_c0c, 1)
            act.wait_ge(s_nm2, 1)
            norm2((0, 0), 0)
            norm2((0, 0), 2)
            hi_x2((0, 0))
            half = NE // 2

            def hi_weights(raw, hi, loaded):
                act.wait_ge(loaded, 32)
                for m in range(2):
                    sl = slice(m * half, (m + 1) * half)
                    nc.scalar.activation(hi[:, sl, :].rearrange("p e h -> p (e h)"),
                                         raw[:, sl, :].rearrange("p e h -> p (e h)"), ACT.Copy).then_inc(s_whi, 1)

            exps((0, 0))
            hi_weights(W1n, W1h, s_w1)
            copy_gates((0, 0))
            for m in range(0, NMAT // TI, 2):
                act.wait_ge(s_ctp, m + 1)
                nc.scalar.activation(ctxT[:, m * TI:(m + 1) * TI, :].rearrange("p m o -> p (m o)"), z[m % NZ][:, :],
                                     ACT.Copy).then_inc(s_ctA, 1)
            hi_weights(W2n, W2h, s_w2)
            act.wait_ge(s_nm1, 2)
            act.wait_ge(s_t1, 1)
            norm1((0, 1), 0)
            norm1((0, 1), 2)
            copy_xnT((0, 1))
            experts((0, 0), plan((0, 0)))
            with act.Fori(0, LOOPS) as k:
                for r in (1, 2):
                    experts((k, r), plan((k, r)))
            for n, c in enumerate(TAIL):
                experts(c, plan(c, len(TAIL) - n))
            copy_y(c)

        @block.vector
        def _(dve):
            def means(stats, mv, veps, first, n, bn, ag, ve, turn, filled=False):
                if filled:
                    dve.wait_ge(s_fill, 2)
                dve.wait_ge(bn, turn)
                for i in range(first, first + n):
                    last = nc.vector.bn_aggr(mv[:, i, :], stats[:, i, :])
                last.then_inc(ag, 1)
                dve.wait_ge(ag, turn)
                nc.vector.tensor_scalar_add(veps[:, first:first + n], mv[:, first:first + n, 1], EPS).then_inc(ve, 1)

            def shifts(mv, rstd, nmr, first, n, rsd, nm, turn):
                dve.wait_ge(rsd, turn)
                nc.vector.scalar_tensor_tensor(nmr[:, first:first + n], mv[:, first:first + n, 0], -1.0,
                                               rstd[:, first:first + n], ALU.mult, ALU.mult).then_inc(nm, 1)

            def stats1_of(first, n, turn):
                dve.wait_ge(s_x[turn - 1], 16 * Q)
                for i in range(first, first + n):
                    last = nc.vector.bn_stats(stats1[:, i, :], xs[:, i, :])
                last.then_inc(s_bn, 1)
                means(stats1, mv1, veps1, first, n, s_bn, s_ag, s_ve, turn)

            def x_of(c, i=0, n=TI):
                k, r = c
                return xs[:, bass.ds(k * (2 * TI) + (r * TI + i), n), :].rearrange("p i d -> p (i d)")

            def add_cross(c):
                dve.wait_ge(s_att, count(c, 1, 1))
                if c[1] > 0:
                    dve.wait_ge(s_xn, count(c, 2, 2))
                nc.vector.scalar_tensor_tensor(x_of(c), att[:, :], tg[:, 0:1], x_of(c), ALU.mult, ALU.add)\
                  .then_inc(s_x1, 1)

            def stats2_of(c, i0):
                for i in (i0, i0 + 1):
                    last = nc.vector.bn_stats(stats2[:, i, :], x_of(c, i, 1))
                last.then_inc(s_bn2, 1)

            def lo_x2(c):
                p = c[1] % 2
                dve.wait_ge(s_x2h, count(c, 1, 1))
                nc.vector.tensor_tensor(x2l[p][:, :], tp[:, :], x2h[p][:, :].bitcast(F32),
                                        ALU.subtract).then_inc(s_x2l, 1)

            def over_experts(a):
                return a[:, :].unsqueeze(2).to_broadcast([P, TI, E])

            def shift_logits(c):
                dve.wait_ge(s_lg, count(c, 1, 1))
                if c[1] > 0:
                    dve.wait_ge(s_exp, count(c, 1))
                nc.vector.tensor_tensor(lg[:, :, :], misc[:, 0:TI * NE].rearrange("p (i e) -> p i e", i=TI)[:, :, 0:E],
                                        rb[:, :].unsqueeze(1).to_broadcast([P, TI, E]), ALU.add).then_inc(s_lb, 1)
                dve.wait_ge(s_lb, count(c, 1, 1))
                nc.vector.reduce_max(mx[:, :], lg[:, :, :], AX.X).then_inc(s_mx, 1)
                dve.wait_ge(s_mx, count(c, 1, 1))
                nc.vector.tensor_tensor(lg[:, :, :], lg[:, :, :], over_experts(mx), ALU.subtract).then_inc(s_sub, 1)

            def choose(c):
                dve.wait_ge(s_exp, count(c, 1, 1))
                nc.vector.reduce_sum(sm[:, :], ex[:, :, :], AX.X).then_inc(s_sm, 1)
                dve.wait_ge(s_sm, count(c, 1, 1))
                nc.vector.reciprocal(rs[:, :], sm[:, :]).then_inc(s_rc, 1)
                dve.wait_ge(s_rc, count(c, 1, 1))
                nc.vector.tensor_tensor(pr[:, :, 0:E], ex[:, :, :], over_experts(rs), ALU.mult).then_inc(s_pr, 1)
                dve.wait_ge(s_fill, 2)
                dve.wait_ge(s_pr, count(c, 1, 1))
                for i in range(TI):
                    last = nc.vector.max(top[:, i, :], pr[:, i, 0:E])
                last.then_inc(s_top, 1)
                dve.wait_ge(s_top, count(c, 1, 1))
                nc.vector.memset(top[:, :, TOPK:8], -1.0).then_inc(s_low, 1)
                dve.wait_ge(s_fill, 2)
                dve.wait_ge(s_low, count(c, 1, 1))
                for i in range(TI):
                    last = nc.vector.match_replace(rest[:, i, :], top[:, i, :], pr[:, i, :], 0.0)
                last.then_inc(s_mr, 1)
                dve.wait_ge(s_mr, count(c, 1, 1))
                if c[1] > 0:
                    dve.wait_ge(s_t3, count(c, 1))
                nc.vector.tensor_tensor(cw[:, :, 0:E], pr[:, :, 0:E], rest[:, :, 0:E], ALU.subtract).then_inc(s_cw, 1)

            def add_y(c):
                k, r = c
                p = r % 2
                dve.wait_ge(s_t4, count(c, 1, 1))
                if r >= 2:
                    dve.wait_ge(s_out[p], count_slot(before(c, 2), 16 * Q))
                nc.vector.scalar_tensor_tensor(ob[p][:, :, :].rearrange("p i d -> p (i d)"), misc[:, :], tg[:, 1:2],
                                               x_of(c), ALU.mult, ALU.add).then_inc(s_fin, 1)

            def scale(c, u):
                n = u % NT
                k, r = c
                dve.wait_ge(s_z, count(c, NE, u + 1))
                if r > 0 or u >= NT:
                    v = (u - NT) % NE
                    of = c if u >= NT else before(c)
                    dve.wait_ge(s_hi, count(c, NE, u + 1 - NT))
                    if v in POOL_LO:
                        dve.wait_ge(s_loP, lo_count(of, v, POOL_LO))
                    else:
                        dve.wait_ge(s_loD, lo_count(of, v, DVE_LO))
                if u == 0:
                    nc.vector.tensor_scalar(t[n][:, :], z[u % NZ][:, :], nb1T[:, 0:1], None, ALU.max).then_inc(s_a, 1)
                    return
                for g, es in enumerate(GROUP):
                    if es[0] == u - 1:
                        dve.wait_ge(s_cwb[r % 2][g], count_slot(c, 16))
                nc.vector.scalar_tensor_tensor(t[n][:, :], z[u % NZ][:, :], nb1T[:, u:u + 1],
                                               cwB[r % 2][:, u - 1, :], ALU.max, ALU.mult).then_inc(s_a, 1)

            def low(c, u):
                n = u % NT
                dve.wait_ge(s_hi, count(c, NE, u + 1))
                if c[1] > 0 or u >= NT:
                    dve.wait_ge(s_h2, count(c, NE, u + 1 - NT))
                nc.vector.tensor_tensor(tl[n][:, :], t[n][:, :], th[n][:, :].bitcast(F32),
                                        ALU.subtract).then_inc(s_loD, 1)

            def aggregate2(c, turn):
                dve.wait_ge(s_fill, 2)
                dve.wait_ge(s_bn2, turn)
                for i in range(TI):
                    last = nc.vector.bn_aggr(mv2[:, i, :], stats2[:, i, :])
                last.then_inc(s_ag2, 1)
                dve.wait_ge(s_ag2, count(c, 1, 1))
                nc.vector.tensor_scalar_add(veps2[:, :], mv2[:, :, 1], EPS).then_inc(s_ve2, 1)

            def experts(c, todo):
                turn = 0
                for u in range(NE):
                    for f, at in todo:
                        if at.get("S2") == u:
                            turn = held(dve, f"ln2_turn{f[1]}", count(f, 2, 2))
                            if at["AX"] < u:
                                dve.wait_ge(s_x1, count(f, 1, 1))
                    scale(c, u)
                    if u == LAG - 1 and c[1] == 0:
                        dve.wait_ge(s_offT, 1)
                        nc.vector.tensor_tensor(offrows[:, :], misc[0:NE, P:2 * P], b2rows[:, :], ALU.add)\
                          .then_inc(s_offr, 1)
                    if u - 1 in DVE_LO:
                        low(c, u - 1)
                    for f, at in todo:
                        if at.get("AX") == u:
                            add_cross(f)
                            if at["S2"] == u:
                                dve.wait_ge(s_x1, count(f, 1, 1))
                        if at.get("S2") == u:
                            stats2_of(f, 0)
                        if at.get("S2") == u - 1:
                            stats2_of(f, 2)
                            aggregate2(f, turn)
                        if at.get("NM") == u:
                            shifts(mv2, rstd2, nmr2, 0, TI, s_rs2, s_nm2, count(f, 1, 1))
                        if at.get("LO") == u:
                            lo_x2(f)
                        if at.get("SH") == u:
                            shift_logits(f)
                        if at.get("CH") == u:
                            choose(f)
                    if u == AY and c[1] > 0:
                        add_y(before(c))
                if NE - 1 in DVE_LO:
                    low(c, NE - 1)

            dve.wait_ge(s_idx, 16)
            nc.vector.tensor_scalar(idx_neg[:, :], idx_raw[:, :], 0.0, float(NMAT), ALU.is_lt, ALU.mult).then_inc(s_idv, 1)
            dve.wait_ge(s_idv, 1)
            nc.vector.tensor_tensor(idx_raw[:, :], idx_raw[:, :], idx_neg[:, :], ALU.add).then_inc(s_idv, 1)
            dve.wait_ge(s_idv, 2)
            nc.vector.tensor_scalar(idx[:, :], idx_raw[:, :], 0.0, float(NMAT - 1), ALU.max, ALU.min).then_inc(s_idxok, 1)
            stats1_of(0, TI, 1)
            shifts(mv1, rstd1, nmr1, 0, TI, s_rs1, s_nm1, 1)
            nc.vector.memset(rW[:, E:NE], 0.0).then_inc(s_rwpad, 1)
            dve.wait_ge(s_rwpad, 1)
            dve.wait_ge(s_rw, 32)
            nc.vector.tensor_copy(rWh[:, :], rW[:, :]).then_inc(s_wrest, 1)
            dve.wait_ge(s_wrest, 1)
            nc.vector.tensor_tensor(rWl[:, :], rW[:, :], rWh[:, :].bitcast(F32), ALU.subtract).then_inc(s_wrest, 1)
            dve.wait_ge(s_b1T, 1)
            nc.vector.tensor_copy(b1T[:, :], misc[:, 0:NE]).then_inc(s_b1c, 1)
            nc.vector.tensor_scalar(nb1T[:, 0:1], misc[:, E:NE], -1.0, None, ALU.mult)
            nc.vector.tensor_scalar(nb1T[:, 1:NE], misc[:, 0:E], -1.0, None, ALU.mult).then_inc(s_b1c, 1)
            dve.wait_ge(s_tg, 1)
            dve.wait_ge(s_xn, 2)
            add_cross((0, 0))
            dve.wait_ge(s_x1, 1)
            stats2_of((0, 0), 0)
            stats2_of((0, 0), 2)
            aggregate2((0, 0), 2)
            shifts(mv2, rstd2, nmr2, 0, TI, s_rs2, s_nm2, 1)
            lo_x2((0, 0))
            dve.wait_ge(s_fill, 2)
            shift_logits((0, 0))
            choose((0, 0))
            for m in range(1, NMAT // TI, 2):
                dve.wait_ge(s_ctp, m + 1)
                nc.vector.tensor_copy(ctxT[:, m * TI:(m + 1) * TI, :].rearrange("p m o -> p (m o)"), z[m % NZ][:, :])\
                  .then_inc(s_ctD, 1)
            half = NE // 2
            for m in range(2):
                dve.wait_ge(s_whi, m + 1)
                sl = slice(m * half, (m + 1) * half)
                nc.vector.tensor_tensor(W1l[:, sl, :], W1n[:, sl, :], W1h[:, sl, :].bitcast(F32),
                                        ALU.subtract).then_inc(s_wlo, 1)
            stats1_of(TI, NTILE - TI, 2)
            dve.wait_ge(s_off, 1)
            nc.vector.tensor_copy(offT[:, :], misc[:, 0:NE]).then_inc(s_offc, 1)
            shifts(mv1, rstd1, nmr1, TI, NTILE - TI, s_rs1, s_nm1, 2)
            experts((0, 0), plan((0, 0)))
            with dve.Fori(0, LOOPS) as k:
                for r in (1, 2):
                    experts((k, r), plan((k, r)))
            for n, c in enumerate(TAIL):
                experts(c, plan(c, len(TAIL) - n))
            add_y(c)


_INS = ['x', 'itok_S_0_31', 'ctx_1024', 'g_xattn', 'g_ffn', 'L0_ffn_router_W', 'L0_ffn_router_b', 'L0_ffn_sW1',
        'L0_ffn_sb1', 'L0_ffn_sW2', 'L0_ffn_sb2', 'L0_ffn_eW1', 'L0_ffn_eb1', 'L0_ffn_eW2', 'L0_ffn_eb2']


def kernel(**inputs):
    import numpy as _np
    import concourse.bacc as _bacc
    from concourse import mybir as _mybir
    from concourse.bass_utils import run_bass_kernel_spmd as _run

    nc = _bacc.Bacc("TRN2", target_bir_lowering=False, num_devices=1)
    arrays, args = {}, []
    for name in _INS:
        a = _np.ascontiguousarray(inputs[name])
        arrays[f"in_{name}"] = a
        args.append(nc.dram_tensor(f"in_{name}", a.shape, _mybir.dt.from_np(a.dtype), kind="ExternalInput").ap())
    x = arrays["in_x"]
    out = nc.dram_tensor("out_dram", x.shape, _mybir.dt.from_np(x.dtype), kind="ExternalOutput").ap()
    gated_moe_block(nc, *args, out)
    r = _run(nc, [arrays], core_ids=[0])
    return r.results[0]["out_dram"]
```

```python
import numpy as np
import concourse.bass as bass
from concourse import mybir
from contextlib import ExitStack

F32 = mybir.dt.float32
F32R = mybir.dt.float32r
I32 = mybir.dt.int32
ALU = mybir.AluOpType
ACT = mybir.ActivationFunctionType
AX = mybir.AxisListType

EPS = 1e-5
TOPK = 3


def count(chunk, per, plus=0):
    k, r = chunk
    return k * (2 * per) + (r * per + plus)


def count_slot(chunk, per):
    k, r = chunk
    return k * per + ((r // 2 + 1) * per)


def held(eng, name, value):
    if isinstance(value, int):
        return value
    reg = eng.alloc_register(name)
    eng.reg_mov(reg, value)
    return reg


def before(chunk, n=1):
    return (chunk[0], chunk[1] - n)


def after(chunk):
    return (chunk[0], chunk[1] + 1)


def gated_moe_block(nc, x, itok, ctx_w, g_xattn, g_ffn, router_W, router_b, sW1, sb1, sW2, sb2,
                    eW1, eb1, eW2, eb2, out):
    NB, S, D = x.shape
    NMAT = ctx_w.shape[0]
    E = router_W.shape[1]
    NE = E + 1
    Q = 4
    TI = 4
    CS = Q * TI
    C = CS * NB
    NCHUNK = S // CS
    P = 128
    H = sW1.shape[1]
    assert D == P and H == P and NB == 32 and NCHUNK % 2 == 0
    NZ = 4
    NT = 8
    LAG = 5
    A_USUAL = dict(N1=0, T1=3, XT=3, CR=4, AX=5, S2=7, RS=9, NM=10, N2=10)
    B_USUAL = dict(T2=0, H2=0, LO=1, RT=3, SH=4, EX=4, CH=5, T3=9, CG=8)
    A_FIRST = dict(A_USUAL, N1=2, T1=5, XT=5, CR=6, AX=7, S2=8, RS=10, NM=11, N2=11)
    SPREAD_AT = {0: (0, 1), 1: (2,), 2: (3,), 3: (4,), 4: (5,)}
    B_FIRST = dict(NM=0, T2=2, H2=1, LO=2, RT=4, SH=4, EX=4, CH=5, T3=9, CG=8)
    TY, YC, AY = 6, LAG - 1, 7

    def plan(c, last=NCHUNK):
        one, two = after(c), after(after(c))
        return [(one, B_USUAL if c[1] > 0 else B_FIRST)] * (last > 1) + [(two, A_USUAL if c[1] > 0 else A_FIRST)] * (last > 2)

    CTX_LOADS = 4
    CTX_PE, CTX_ACT, CTX_DVE = 6, 4, 2
    LN1 = [(n, 1) for n in range(NCHUNK)]
    LATE = {3 + n: dict(stats=[s], mean=s + 1, rsqrt=s + 2, shift=s + 4) for n, s in enumerate((2, 4, 6, 9, 11))}
    EARLY = 10
    SPACED = 1
    DIRECT = 2
    BW = 32
    CG = 4
    GROUP = [range(0, 2), range(2, 6), range(6, 10), range(10, 15)]
    DIRECTLY = range(0, GROUP[DIRECT - 1][-1] + 1)
    PADK = TOPK + 5
    EW = E + 5

    DVE_LO = [1, 5, 9, 13]
    POOL_LO = [u for u in range(NE) if u not in DVE_LO]

    def lo_count(chunk, u, mine):
        return count(chunk, len(mine), len([v for v in mine if v <= u]))

    ctx = ExitStack()
    with ctx:
        def sb(name, shape, dt=F32):
            return ctx.enter_context(nc.sbuf_tensor(name, shape, dt))

        def ps(name, shape):
            return ctx.enter_context(nc.psum_tensor(name, shape, F32))

        def sem(name):
            return ctx.enter_context(nc.semaphore(name))

        scratch = nc.dram_tensor("gates_scratch", (NCHUNK, E, C), F32, kind="Internal").ap()

        ident = sb("ident", [P, P])
        ctxT = sb("ctxT", [P, NMAT, P])
        W1h, W1l = sb("W1h", [P, NE, H], F32R), sb("W1l", [P, NE, H], F32R)
        W2h, W2l = sb("W2h", [P, NE, D], F32R), sb("W2l", [P, NE, D], F32R)
        W2n = sb("W2n", [P, NE, D])
        rWs = sb("rWs", [P, 2, NE], F32R)
        rW = sb("rW", [P, NE])
        rb = sb("rb", [P, E])
        idx_raw, idx_neg, idx = sb("idx_raw", [1, S], I32), sb("idx_neg", [1, S], I32), sb("idx", [1, S], I32)
        gates_in, tg = sb("gates_in", [P, 2]), sb("tg", [P, 2])
        b1rows, b2rows, offS = sb("b1rows", [NE, H]), sb("b2rows", [NE, D]), sb("offS", [2 * BW + NE, D], F32R)
        bT, nb1T, offT = sb("bT", [P, 2, NE]), sb("nb1T", [P, NE]), sb("offT", [P, NE])
        offX = sb("offX", [P, 3, BW])
        sel = sb("sel", [2 * BW + NE, NE], F32R)
        NTILE = NCHUNK * TI
        xs = sb("xs", [P, NTILE, D])
        xn = sb("xn", [P, TI, D])
        xn2 = sb("xn2", [P, TI, D])
        xnT = sb("xnT", [P, TI, P])
        Wg = [sb(f"Wg{p}", [P, CS, P]) for p in range(2)]
        x2h = [sb(f"x2h{p}", [P, C], F32R) for p in range(2)]
        x2l = [sb(f"x2l{p}", [P, C], F32R) for p in range(2)]
        stat1, mv1 = sb("stat1", [P, NTILE, 6]), sb("mv1", [P, NTILE, 2])
        veps1, rstd1, nmr1 = sb("veps1", [P, NTILE]), sb("rstd1", [P, NTILE]), sb("nmr1", [P, NTILE])
        stats2, mv2 = sb("stats2", [P, TI, 6]), sb("mv2", [P, TI, 2])
        veps2, rstd2, nmr2 = sb("veps2", [P, TI]), sb("rstd2", [P, TI]), sb("nmr2", [P, TI])
        mhalf = sb("mhalf", [P, NTILE])
        lg = sb("lg", [P, TI, E])
        ex = sb("ex", [P, TI, E])
        mx, sm, rs = sb("mx", [P, TI]), sb("sm", [P, TI]), sb("rs", [P, TI])
        pr = sb("pr", [P, TI, EW])
        rest = sb("rest", [P, TI, EW])
        top = sb("top", [P, TI, 8])
        cw = sb("cw", [P, TI, 4, BW])
        cwT = [sb(f"cwT{p}", [3 * BW + NE, C]) for p in range(2)]
        cwS = [sb(f"cwS{p}", [2 * BW + NE, C], F32R) for p in range(2)]
        cwB = sb("cwB", [P, E, C])
        tall = sb("t", [P, NT, C])
        t = [tall[:, n, :] for n in range(NT)]
        th = [sb(f"th{n}", [P, C], F32R) for n in range(NT)]
        tl = [sb(f"tl{n}", [P, C], F32R) for n in range(NT)]
        ysb = sb("ysb", [P, C])
        ob = [sb(f"ob{p}", [P, TI, D]) for p in range(2)]
        early = cwB[:, :, :].rearrange("p e c -> p (e c)")
        ctxn = early[:, 0:NMAT * P].rearrange("p (m d) -> p m d", m=NMAT)
        xnT0 = tall[:, :, :].rearrange("p n c -> p (n c)")[:, 0:TI * Q * P].rearrange("p (i q t) -> p i q t", i=TI, q=Q)
        W1n = early[:, NMAT * P:NMAT * P + NE * H].rearrange("p (e h) -> p e h", e=NE)

        z = [ps(f"z{n}", [P, C]) for n in range(NZ)]
        y = ps("y", [P, C])
        tp = ps("tp", [P, C])
        att = ps("att", [P, C])
        misc = ps("misc", [P, C])
        direct_bank = [y, att]

        s_idx, s_gate, s_bias, s_w1, s_w2, s_rw = (sem(n) for n in
            ("idx_loaded", "g_loaded", "bias_loaded", "W1_loaded", "W2_loaded", "router_loaded"))
        s_ctx = [sem(f"ctx_loaded{n}") for n in range(CTX_LOADS)]
        s_x = [sem("x_first_loaded"), sem("x_second_loaded"), sem("x_rest_loaded")]
        s_wg = [sem(f"gathered{p}") for p in range(2)]
        s_scr = sem("gates_written")
        s_cwb = [sem(f"gates_spread{g}") for g in range(CG)]
        s_out = [sem(f"out_stored{p}") for p in range(2)]
        s_ident, s_idv, s_idxok, s_rwpad, s_tg = (sem(n) for n in
            ("ident_made", "idx_step", "idx_ready", "router_padded", "tanh_ready"))
        s_ctp, s_ctA, s_ctD = sem("ctx_transposed"), sem("ctx_copied_scalar"), sem("ctx_copied_vector")
        s_b1T, s_b1c, s_off, s_offc, s_offT, s_offr = (sem(n) for n in
            ("b1_transposed", "b1_copied", "off_summed", "off_copied", "off_transposed", "off_ready"))
        s_whi, s_wlo, s_w2lo, s_wrest = (sem(n) for n in ("W_hi_made", "W1_lo_made", "W2_lo_made", "rW_split"))
        s_zero = sem("zeros_set")
        s_fill, s_mh = sem("fillers_set"), sem("minus_half_set")
        s_bn, s_ag, s_ve, s_rs1, s_nm1, s_xn = (sem(n) for n in
            ("ln1_stats", "ln1_meanvar", "ln1_var_eps", "ln1_rstd", "ln1_shift", "ln1_done"))
        s_bn2, s_ag2, s_ve2, s_rs2, s_nm2, s_xn2 = (sem(n) for n in
            ("ln2_stats", "ln2_meanvar", "ln2_var_eps", "ln2_rstd", "ln2_shift", "ln2_done"))
        s_t1, s_e1, s_att, s_x1, s_t2, s_x2h, s_x2l = (sem(n) for n in
            ("xn_transposed", "xnT_copied", "att_done", "x1_ready", "xn2_transposed", "x2_hi", "x2_lo"))
        s_lg, s_lb, s_mx, s_sub, s_exp, s_sm, s_rc, s_pr, s_top, s_low, s_mr, s_cw = (sem(n) for n in
            ("logits", "logits_biased", "logit_max", "logits_shifted", "exps", "exp_sum", "exp_sum_inv",
             "probs", "top8", "top3", "top_removed", "gates"))
        s_t3, s_cwT, s_cwS = sem("gates_transposed"), sem("gatesT_copied"), sem("gatesT_parts_copied")
        s_sel, s_bc, s_bcc = sem("selector_made"), sem("gates_spread_by_pe"), sem("gates_spread_copied")
        s_cwf, s_cwh = sem("gates_whole"), sem("gates_hi")
        s_offh, s_off2 = sem("off_hi"), sem("off_whole")
        s_z, s_a, s_hi, s_loP, s_loD, s_h2 = (sem(n) for n in
            ("z_done", "t_ready", "t_hi", "t_lo_pool", "t_lo_vector", "y_added"))
        s_y, s_ys, s_t4, s_fin = (sem(n) for n in ("y_done", "y_copied", "y_transposed", "out_ready"))

        block = ctx.enter_context(nc.Block())
        LOOPS = (NCHUNK - 4) // 2
        TAIL = [(LOOPS, 1), (LOOPS, 2), (LOOPS, 3)]

        def load_x(eng, c0, c1, loaded, quarters=range(Q)):
            for q in quarters:
                rows = x.rearrange("b (c q i) d -> q b c (i d)", q=Q, i=TI)[q, :, c0:c1, :]
                eng.dma_start(xs[32 * q:32 * q + 32, c0 * TI:c1 * TI, :].rearrange("p (c i) d -> p c (i d)", i=TI),
                              rows).then_inc(loaded, 16)

        @block.sync
        def _(sp):
            def matrices_of(c):
                k, r = c
                return nc.values_load_multi_w_load_instructions(
                    idx[0:1, bass.ds(k * (2 * CS) + r * CS, CS)], engines=(sp.engine,), min_val=0, max_val=NMAT - 1,
                    skip_runtime_bounds_check_because="brought into range on the chip")[1]

            def gather(c, at, own=range(CS)):
                k, r = c
                if r >= 3 and own[0] == 0:
                    sp.wait_ge(s_att, count(before(c, 2), 1, 1))
                if r == 1:
                    sp.wait_ge(s_ctA, NMAT // TI // 2)
                    sp.wait_ge(s_ctD, NMAT // TI // 2)
                for n in own:
                    sp.dma_start(Wg[r % 2][:, n, :],
                                 ctxT[:, bass.ds(at[n], 1), :].rearrange("p a o -> p (a o)"))\
                      .then_inc(s_wg[r % 2], 16)

            def write_gates(c):
                k, r = c
                sp.wait_ge(s_cwT, count(c, 1, 1))
                sp.dma_start(scratch[bass.ds(k * 2 + r, 1), :, :].rearrange("a e c -> (a e) c"),
                             cwT[r % 2][3 * BW:3 * BW + E, :]).then_inc(s_scr, 16)

            def spread_gates(c, groups=range(CG)):
                k, r = c
                start = groups[0] == (DIRECT if r == 0 else 0)
                if start:
                    written = held(sp, f"written{r}", count(c, 16, 16))
                used = [held(sp, f"used{r}_{g}", count(before(c), NE, GROUP[g][-1] + 2)) if r >= 1 else 0
                        for g in groups]
                if r == 0:
                    sp.wait_ge(s_wlo, 2)
                    sp.wait_ge(s_ctp, NMAT // TI)
                if start:
                    sp.wait_ge(s_scr, written)
                for g, u in zip(groups, used):
                    es = GROUP[g]
                    if r >= 1:
                        sp.wait_ge(s_a, u)
                    src = scratch[bass.ds(k * 2 + r, 1), es[0]:es[-1] + 1, :].rearrange("a e c -> (a e c)")
                    sp.dma_start(cwB[:, es[0]:es[-1] + 1, :].rearrange("p e c -> p (e c)"),
                                 src.partition_broadcast(P)).then_inc(s_cwb[g], 16)

            def store(c):
                k, r = c
                sp.wait_ge(s_fin, count(c, 1, 1))
                for q in range(Q):
                    rows = out[:, bass.ds(k * (2 * CS) + (r * CS + TI * q), TI), :]
                    sp.dma_start(rows.rearrange("b i d -> b (i d)"),
                                 ob[r % 2][32 * q:32 * q + 32, :, :].rearrange("p i d -> p (i d)"))\
                      .then_inc(s_out[r % 2], 16)

            load_x(sp, 0, 1, s_x[0], range(0, 2))
            per = NMAT // CTX_LOADS
            for n in range(CTX_LOADS):
                sp.dma_start(ctxn[:, n * per:(n + 1) * per, :],
                             ctx_w[n * per:(n + 1) * per].rearrange("m o d -> o m d")).then_inc(s_ctx[n], 16)
            sp.dma_start(b1rows[0:E, :], eb1).then_inc(s_bias, 16)
            sp.dma_start(b1rows[E:NE, :], sb1.rearrange("(a n) -> a n", a=1)).then_inc(s_bias, 16)
            sp.dma_start(b2rows[0:E, :], eb2).then_inc(s_bias, 16)
            sp.dma_start(b2rows[E:NE, :], sb2.rearrange("(a n) -> a n", a=1)).then_inc(s_bias, 16)
            sp.dma_start(rW[:, 0:E], router_W).then_inc(s_rw, 16)
            sp.dma_start(rb[:, :], router_b.partition_broadcast(P)).then_inc(s_rw, 16)
            sp.dma_start(W1n[:, 0, :], sW1).then_inc(s_w1, 16)
            sp.dma_start(W1n[:, 1:NE, :], eW1.rearrange("e d h -> d e h")).then_inc(s_w1, 16)
            load_x(sp, 1, 2, s_x[1])
            sp.dma_start(W2n[:, 0, :], sW2).then_inc(s_w2, 16)
            sp.dma_start(W2n[:, 1:NE, :], eW2.rearrange("e h d -> h e d")).then_inc(s_w2, 16)
            load_x(sp, 2, NCHUNK, s_x[2])
            sp.wait_ge(s_idxok, 1)
            gather((0, 1), matrices_of((0, 1)))
            at = matrices_of((0, 2))
            gather((0, 2), at, range(0, EARLY))
            write_gates((0, 0))
            gather((0, 2), at, range(EARLY, CS))
            spread_gates((0, 0), range(DIRECT, CG))

            def beside(c, left=NCHUNK):
                if left > 3:
                    at = matrices_of(after(after(after(c))))
                    gather(after(after(after(c))), at, range(0, CS // 2))
                if c[1] > 0:
                    store(before(c))
                if left > 1:
                    write_gates(after(c))
                    spread_gates(after(c), range(0, CG - 1))
                if left > 3:
                    gather(after(after(after(c))), at, range(CS // 2, CS))
                if left > 1:
                    spread_gates(after(c), range(CG - 1, CG))

            beside((0, 0))
            with sp.Fori(0, LOOPS) as k:
                for r in (1, 2):
                    beside((k, r))
            for n, c in enumerate(TAIL[:-1]):
                beside(c, len(TAIL) - n)
            store(before(TAIL[-1]))
            store(TAIL[-1])
            for p in range(2):
                sp.wait_ge(s_out[p], 16 * Q * (NCHUNK // 2))

        @block.gpsimd
        def _(pool):
            pool.memset(ident[:, :], 0.0).then_inc(s_ident, 1)
            pool.wait_ge(s_ident, 1)
            pool.affine_select(out=ident[:, :], in_=ident[:, :], compare_op=ALU.not_equal, fill=1.0,
                               base=0, pattern=[[-1, P]], channel_multiplier=1).then_inc(s_ident, 1)
            pool.wait_ge(s_ident, 2)
            pool.tensor_tensor(sel[:, :], ident[0:2 * BW + NE, 0:NE], ident[0:2 * BW + NE, 2 * BW:2 * BW + NE],
                               ALU.add).then_inc(s_sel, 1)
            pool.memset(cw[:, :, :, :], 0.0).then_inc(s_mh, 1)
            pool.memset(offX[:, :, :], 0.0).then_inc(s_zero, 1)
            pool.wait_ge(s_mh, 1)
            pool.memset(cw[:, :, 0:2, E:NE], 1.0)
            pool.memset(cw[:, :, 3, E:NE], 1.0).then_inc(s_fill, 1)
            pool.memset(pr[:, :, E:EW], -1.0).then_inc(s_fill, 1)
            pool.memset(mhalf[:, :], -0.5).then_inc(s_mh, 1)
            pool.memset(xnT0[:, :, :, :], 0.0).then_inc(s_zero, 1)
            pool.wait_ge(s_mh, 2)

            def rsqrt(veps, rstd, ve, rsd, turn):
                pool.wait_ge(ve, turn)
                pool.tensor_tensor(rstd, veps, mhalf[:, 0:veps.shape[-1]], ALU.pow).then_inc(rsd, 1)


            def rsqrt1(turn):
                first, n = LN1[turn]
                sl = slice(first * TI, (first + n) * TI)
                rsqrt(veps1[:, sl], rstd1[:, sl], s_ve, s_rs1, turn + 1)

            rsqrt1(0)
            rsqrt1(1)

            def lo_w2(m):
                sl = slice(m * NE // 2, (m + 1) * NE // 2)
                pool.wait_ge(s_whi, m + 3)
                pool.tensor_tensor(W2l[:, sl, :], W2n[:, sl, :], W2h[:, sl, :].bitcast(F32),
                                   ALU.subtract).then_inc(s_w2lo, 1)

            rsqrt(veps2[:, :], rstd2[:, :], s_ve2, s_rs2, 1)
            lo_w2(0)
            lo_w2(1)
            rsqrt1(2)
            rsqrt(veps2[:, :], rstd2[:, :], s_ve2, s_rs2, 2)

            def experts(c, todo):
                for u in range(NE):
                    for f, at in todo:
                        if at.get("RS") == u:
                            rsqrt(veps2[:, :], rstd2[:, :], s_ve2, s_rs2, count(f, 1, 1))
                    for turn, at in LATE.items():
                        if c[1] == 0 and at["rsqrt"] == u:
                            rsqrt1(turn)
                    if u not in POOL_LO:
                        continue
                    n = u % NT
                    pool.wait_ge(s_hi, count(c, NE, u + 1))
                    if c[1] > 0 or u >= NT:
                        pool.wait_ge(s_h2, count(c, NE, u + 1 - NT))
                    pool.tensor_tensor(tl[n][:, :], t[n], th[n][:, :].bitcast(F32),
                                       ALU.subtract).then_inc(s_loP, 1)

            experts((0, 0), plan((0, 0)))
            with pool.Fori(0, LOOPS) as k:
                for r in (1, 2):
                    experts((k, r), plan((k, r)))
            for n, c in enumerate(TAIL):
                experts(c, plan(c, len(TAIL) - n))

        @block.tensor
        def _(pe):
            def product(ps_out, wh, wl, xh, xl, start, stop, inc=None):
                nc.tensor.matmul(ps_out, wh, xh, start=start, stop=False)
                nc.tensor.matmul(ps_out, wh, xl, start=False, stop=False)
                return nc.tensor.matmul(ps_out, wl, xh, start=False, stop=stop)

            def transpose_xn(c):
                if c[1] > 1:
                    pe.wait_ge(s_x2h, count(c, 1))
                    pe.wait_ge(s_x2l, count(c, 1))
                elif c[1] == 1:
                    pe.wait_ge(s_e1, 1)
                pe.wait_ge(s_xn, count(c, 2, 2))
                for i in range(TI):
                    mm = nc.tensor.transpose(tp[:, i * P:(i + 1) * P], xn[:, i, :], ident[:, :])
                mm.then_inc(s_t1, 1)

            def cross(c):
                pe.wait_ge(s_e1, count(c, 1, 1))
                if c[1] % 2:
                    pe.wait_ge(s_wg[1], count_slot(c, 16 * CS))
                else:
                    pe.wait_ge(s_wg[0], count_slot(before(c, 2), 16 * CS))
                pe.wait_ge(s_x1, count(c, 1))
                if c[1] > 1:
                    pe.wait_ge(s_cwS, count(before(c), 1))
                if c[1] == 2:
                    pe.wait_ge(s_bcc, 6)
                for i in range(TI):
                    for q in range(Q):
                        mm = nc.tensor.matmul(att[32 * q:32 * q + 32, i * D:(i + 1) * D],
                                              xnT[:, i, 32 * q:32 * q + 32], Wg[c[1] % 2][:, TI * q + i, :],
                                              start=True, stop=True)
                mm.then_inc(s_att, 1)

            def cross_first():
                pe.wait_ge(s_e1, 1)
                pe.wait_ge(s_ctA, NMAT // TI // 2)
                pe.wait_ge(s_ctD, NMAT // TI // 2)
                for i in range(TI):
                    for q in range(Q):
                        mm = nc.tensor.matmul(att[:, i * D:(i + 1) * D], xnT0[:, i, q, :],
                                              ctxT[:, bass.ds(at[TI * q + i], 1), :].rearrange("p a o -> p (a o)"),
                                              start=q == 0, stop=q == Q - 1)
                mm.then_inc(s_att, 1)

            def transpose_xn2(c):
                if c[1] == 0:
                    pe.wait_ge(s_e1, 2)
                if c[1] == 1:
                    pe.wait_ge(s_cwS, 1)
                pe.wait_ge(s_xn2, count(c, 2, 2))
                for i in range(TI):
                    mm = nc.tensor.transpose(tp[:, i * P:(i + 1) * P], xn2[:, i, :], ident[:, :])
                mm.then_inc(s_t2, 1)

            def router(c):
                p = c[1] % 2
                pe.wait_ge(s_x2h, count(c, 1, 1))
                pe.wait_ge(s_x2l, count(c, 1, 1))
                if c[1] == 0:
                    pe.wait_ge(s_wrest, 2)
                if c[1] > 2:
                    pe.wait_ge(s_fin, count(before(c, 2), 1))
                for i in range(TI):
                    sl = slice(i * P, (i + 1) * P)
                    nc.tensor.matmul(misc[:, i * 2 * NE:(i + 1) * 2 * NE], x2h[p][:, sl],
                                     rWs[:, :, :].rearrange("p h e -> p (h e)"), start=True, stop=False)
                    mm = nc.tensor.matmul(misc[:, i * 2 * NE:i * 2 * NE + NE], x2l[p][:, sl], rWs[:, 0, :],
                                          start=False, stop=True)
                mm.then_inc(s_lg, 1)

            def transpose_gates(c, more=True):
                pe.wait_ge(s_cw, count(c, 1, 1))
                bank = att if c[1] > 0 else tp
                if more and c[1] > 0:
                    pe.wait_ge(s_x1, count(c, 1, 2))
                for i in range(TI):
                    mm = nc.tensor.transpose(bank[0:3 * BW + NE, i * P:(i + 1) * P],
                                             cw[:, i, :, :].rearrange("p b e -> p (b e)")[:, 0:3 * BW + NE], ident[:, :])
                mm.then_inc(s_t3, 1)

            def first(c, u):
                p = c[1] % 2
                if u == 0:
                    pe.wait_ge(s_x2l, count(c, 1, 1))
                if c[1] == 0 and u == NZ - 1:
                    pe.wait_ge(s_offr, 1)
                if c[1] > 0 or u >= NZ:
                    pe.wait_ge(s_a, count(c, NE, u + 1 - NZ))
                product(z[u % NZ][:, :], W1h[:, u, :], W1l[:, u, :], x2h[p][:, :], x2l[p][:, :],
                        True, True).then_inc(s_z, 1)

            def second(c, u):
                n = u % NT
                if u == 0 and c[1] > 0:
                    pe.wait_ge(s_ys, count(c, 1))
                if u == 0 and c[1] == 0:
                    pe.wait_ge(s_bcc, 5)
                pe.wait_ge(s_hi, count(c, NE, u + 1))
                if u in POOL_LO:
                    pe.wait_ge(s_loP, lo_count(c, u, POOL_LO))
                else:
                    pe.wait_ge(s_loD, lo_count(c, u, DVE_LO))
                product(y[:, :], W2h[:, u, :], W2l[:, u, :], th[n][:, :], tl[n][:, :],
                        u == 0, False).then_inc(s_h2, 1)

            def spread_directly(e):
                if e == 0:
                    pe.wait_ge(s_sel, 1)
                    pe.wait_ge(s_cwS, 1)
                if e == 1:
                    pe.wait_ge(s_x1, 2)
                if e >= 2:
                    pe.wait_ge(s_bcc, e - 1)
                nc.tensor.matmul(direct_bank[e % 2][:, :], sel[:, e:e + 1].to_broadcast([2 * BW + NE, P]), cwS[0][:, :],
                                 start=True, stop=True).then_inc(s_bc, 1)

            def finish_y(c):
                pe.wait_ge(s_cwS, count(c, 1, 1))
                nc.tensor.matmul(y[:, :], offS[:, :], cwS[c[1] % 2][:, :], start=False, stop=True)\
                  .then_inc(s_y, 1)

            def transpose_y(c, logits_of):
                pe.wait_ge(s_ys, count(c, 1, 1))
                pe.wait_ge(s_lb, count(logits_of, 2, 2))
                for i in range(TI):
                    mm = nc.tensor.transpose(misc[:, i * P:(i + 1) * P], ysb[:, i * P:(i + 1) * P], ident[:, :])
                mm.then_inc(s_t4, 1)

            def transpose_ctx(m):
                pe.wait_ge(s_ctx[m * CTX_LOADS * TI // NMAT], 16)
                if m >= NZ:
                    pe.wait_ge(s_ctD if m % 2 else s_ctA, (m - NZ) // 2 + 1)
                for i in range(TI):
                    mm = nc.tensor.transpose(z[m % NZ][:, i * P:(i + 1) * P], ctxn[:, m * TI + i, :], ident[:, :])
                mm.then_inc(s_ctp, 1)

            pe.wait_ge(s_ident, 2)
            for m in range(CTX_PE):
                transpose_ctx(m)
            transpose_xn((0, 0))
            for m in range(CTX_PE, NMAT // TI):
                transpose_ctx(m)
            pe.wait_ge(s_bias, 64)
            nc.tensor.transpose(misc[:, 0:NE], b1rows[:, :], ident[0:NE, 0:NE])
            nc.tensor.transpose(misc[:, NE:2 * NE], b2rows[:, :], ident[0:NE, 0:NE]).then_inc(s_b1T, 1)
            pe.wait_ge(s_idxok, 1)
            at = nc.values_load_multi_w_load_instructions(
                idx[0:1, 0:CS], engines=(pe.engine,), min_val=0, max_val=NMAT - 1,
                skip_runtime_bounds_check_because="brought into range on the chip")[1]
            cross_first()

            def offsets(es):
                for e in es:
                    mm = nc.tensor.matmul(z[NZ - 1][:, e:e + 1], W2n[:, (e + 1) % NE, :], bT[:, 0, e:e + 1],
                                          start=True, stop=True)
                return mm

            pe.wait_ge(s_w2, 32)
            pe.wait_ge(s_b1c, 2)
            offsets(range(0, NE // 2))
            transpose_xn((0, 1))
            offsets(range(NE // 2, NE)).then_inc(s_off, 1)
            transpose_xn2((0, 0))
            router((0, 0))
            pe.wait_ge(s_offc, 1)
            nc.tensor.transpose(z[NZ - 1][0:2 * BW + NE, 0:P],
                                offX[:, :, :].rearrange("p b e -> p (b e)")[:, 0:2 * BW + NE], ident[:, :]).then_inc(s_offT, 1)
            cross((0, 1))
            transpose_gates((0, 0))
            pe.wait_ge(s_wlo, 2)

            def experts(c, todo, left=NCHUNK):
                for u in range(NE):
                    first(c, u)
                    if c[1] == 0:
                        for e in SPREAD_AT.get(u, ()):
                            spread_directly(e)
                    if u == LAG - 1 and c[1] == 0:
                        pe.wait_ge(s_w2lo, 2)
                    if u >= LAG:
                        second(c, u - LAG)
                    elif c[1] > 0:
                        second(before(c), NE + u - LAG)
                    if u == LAG - 1 and c[1] > 0:
                        finish_y(before(c))
                    for f, at in todo:
                        if at.get("T1") == u:
                            transpose_xn(f)
                        if at.get("CR") == u:
                            cross(f)
                        if at.get("T2") == u:
                            transpose_xn2(f)
                        if at.get("RT") == u:
                            router(f)
                        if at.get("T3") == u:
                            transpose_gates(f, left > 2)
                    if u == TY and c[1] > 0:
                        transpose_y(before(c), after(c) if left > 1 else c)

            experts((0, 0), plan((0, 0)))
            with pe.Fori(0, LOOPS) as k:
                for r in (1, 2):
                    experts((k, r), plan((k, r)))
            for n, c in enumerate(TAIL):
                experts(c, plan(c, len(TAIL) - n), len(TAIL) - n)
            for u in range(NE - LAG, NE):
                second(c, u)
            finish_y(c)
            transpose_y(c, c)

        @block.scalar
        def _(act):
            act.dma_start(idx_raw[:, :], itok.rearrange("(a n) -> a n", a=1)).then_inc(s_idx, 16)
            load_x(act, 0, 1, s_x[0], range(2, Q))
            act.dma_start(gates_in[:, 0:1], g_xattn.partition_broadcast(P)).then_inc(s_gate, 16)
            act.dma_start(gates_in[:, 1:2], g_ffn.partition_broadcast(P)).then_inc(s_gate, 16)

            def norm(c, i0, dst, rstd, nmr, done, dyn):
                k, r = c
                for i in (i0, i0 + 1):
                    at = bass.ds(k * (2 * TI) + (r * TI + i), 1)
                    own = at if dyn else slice(i, i + 1)
                    last = nc.scalar.activation(dst[:, i, :], xs[:, at, :].rearrange("p a d -> p (a d)"),
                                                ACT.Identity, bias=nmr[:, own], scale=rstd[:, own])
                last.then_inc(done, 1)

            def norm1(c, i0):
                norm(c, i0, xn, rstd1, nmr1, s_xn, True)

            def norm2(c, i0):
                norm(c, i0, xn2, rstd2, nmr2, s_xn2, False)

            def copy_xnT(c):
                act.wait_ge(s_t1, count(c, 1, 1))
                if c[1] > 1:
                    act.wait_ge(s_att, count(c, 1))
                nc.scalar.activation(xnT[:, :, :].rearrange("p i t -> p (i t)"), tp[:, :], ACT.Copy).then_inc(s_e1, 1)

            def hi_x2(c):
                act.wait_ge(s_t2, count(c, 1, 1))
                if c[1] > 1:
                    act.wait_ge(s_z, count(before(c), NE))
                nc.scalar.activation(x2h[c[1] % 2][:, :], tp[:, :], ACT.Copy).then_inc(s_x2h, 1)

            def exps(c):
                act.wait_ge(s_sub, count(c, 1, 1))
                nc.scalar.activation(ex[:, :, :].rearrange("p i e -> p (i e)"),
                                     lg[:, :, :].rearrange("p i e -> p (i e)"), ACT.Exp).then_inc(s_exp, 1)

            def copy_gates(c):
                act.wait_ge(s_t3, count(c, 1, 1))
                if c[1] > 1:
                    act.wait_ge(s_y, count(before(c), 1))
                    act.wait_ge(s_scr, count(before(c), 16))
                bank = att if c[1] > 0 else tp
                nc.scalar.activation(cwT[c[1] % 2][3 * BW:3 * BW + NE, :], bank[3 * BW:3 * BW + NE, :], ACT.Copy)\
                  .then_inc(s_cwT, 1)
                nc.scalar.activation(cwS[c[1] % 2][:, :], bank[0:2 * BW + NE, :], ACT.Copy).then_inc(s_cwS, 1)

            def copy_y(c):
                act.wait_ge(s_y, count(c, 1, 1))
                if c[1] > 0:
                    act.wait_ge(s_t4, count(c, 1))
                nc.scalar.activation(ysb[:, :], y[:, :], ACT.Copy).then_inc(s_ys, 1)

            def copy_spread(e):
                act.wait_ge(s_bc, e + 1)
                if e == 0:
                    act.wait_ge(s_wlo, 2)
                    act.wait_ge(s_ctp, NMAT // TI)
                nc.scalar.activation(cwB[:, e, :], direct_bank[e % 2][:, :], ACT.Copy).then_inc(s_bcc, 1)

            def experts(c, todo):
                for u in range(NE):
                    n = u % NT
                    for f, at in todo:
                        if at.get("N1") == u:
                            act.wait_ge(s_t1, count(f, 1))
                        if at.get("N2") == u:
                            act.wait_ge(s_nm2, count(f, 1, 1))
                            act.wait_ge(s_t2, count(f, 1))
                    act.wait_ge(s_a, count(c, NE, u + 1))
                    if c[1] > 0 or u >= NT:
                        act.wait_ge(s_h2, count(c, NE, u + 1 - NT))
                    nc.scalar.activation(th[n][:, :], t[n], ACT.Copy).then_inc(s_hi, 1)
                    if c[1] == 0 and u + 2 in DIRECTLY:
                        copy_spread(u + 2)
                    for f, at in todo:
                        for half in range(2):
                            if at.get("N1") == u - half:
                                norm1(f, 2 * half)
                            if at.get("N2") == u - half:
                                norm2(f, 2 * half)
                        if at.get("XT") == u:
                            copy_xnT(f)
                        if at.get("H2") == u:
                            hi_x2(f)
                        if at.get("EX") == u:
                            exps(f)
                        if at.get("CG") == u:
                            copy_gates(f)
                    if u == YC and c[1] > 0:
                        copy_y(before(c))

            def copy_ctx(m):
                act.wait_ge(s_ctp, m + 1)
                nc.scalar.activation(ctxT[:, m * TI:(m + 1) * TI, :].rearrange("p m o -> p (m o)"), z[m % NZ][:, :],
                                     ACT.Copy).then_inc(s_ctA, 1)

            def hi_weights(raw, hi, loaded, m):
                sl = slice(m * NE // 2, (m + 1) * NE // 2)
                act.wait_ge(loaded, 32)
                nc.scalar.activation(hi[:, sl, :].rearrange("p e h -> p (e h)"),
                                     raw[:, sl, :].rearrange("p e h -> p (e h)"), ACT.Copy).then_inc(s_whi, 1)

            for m in range(0, CTX_ACT, 2):
                copy_ctx(m)
            act.wait_ge(s_nm1, 1)
            norm1((0, 0), 0)
            norm1((0, 0), 2)
            for m in range(CTX_ACT, NMAT // TI, 2):
                copy_ctx(m)
            act.wait_ge(s_t1, 1)
            act.wait_ge(s_zero, 2)
            for q in range(Q):
                own = slice(32 * q, 32 * q + 32)
                last = nc.scalar.activation(xnT0[:, :, q, own], tp[:, :].rearrange("p (i t) -> p i t", i=TI)[:, :, own],
                                            ACT.Copy)
            last.then_inc(s_e1, 1)
            act.wait_ge(s_gate, 32)
            nc.scalar.activation(tg[:, :], gates_in[:, :], ACT.Tanh).then_inc(s_tg, 1)
            hi_weights(W1n, W1h, s_w1, 0)
            hi_weights(W1n, W1h, s_w1, 1)
            act.wait_ge(s_nm1, 2)
            act.wait_ge(s_t1, 1)
            norm1((0, 1), 0)
            norm1((0, 1), 2)
            hi_weights(W2n, W2h, s_w2, 0)
            copy_xnT((0, 1))
            act.wait_ge(s_nm2, 1)
            norm2((0, 0), 0)
            norm2((0, 0), 2)
            hi_x2((0, 0))
            hi_weights(W2n, W2h, s_w2, 1)
            exps((0, 0))
            copy_gates((0, 0))

            copy_spread(0)
            copy_spread(1)
            act.wait_ge(s_nm2, 2)
            act.wait_ge(s_t2, 1)
            norm2((0, 1), 0)
            norm2((0, 1), 2)

            experts((0, 0), plan((0, 0)))
            act.wait_ge(s_nm1, len(LN1))
            with act.Fori(0, LOOPS) as k:
                for r in (1, 2):
                    experts((k, r), plan((k, r)))
            for n, c in enumerate(TAIL):
                experts(c, plan(c, len(TAIL) - n))
            copy_y(c)

        @block.vector
        def _(dve):
            def means(stats, mv, veps, first, n, bn, ag, ve, turn, filled=False):
                if filled:
                    dve.wait_ge(s_fill, 2)
                dve.wait_ge(bn, turn)
                for i in range(first, first + n):
                    last = nc.vector.bn_aggr(mv[:, i, :], stats[:, i, :])
                last.then_inc(ag, 1)
                dve.wait_ge(ag, turn)
                nc.vector.tensor_scalar_add(veps[:, first:first + n], mv[:, first:first + n, 1], EPS).then_inc(ve, 1)

            def shifts(mv, rstd, nmr, first, n, rsd, nm, turn):
                dve.wait_ge(rsd, turn)
                nc.vector.scalar_tensor_tensor(nmr[:, first:first + n], mv[:, first:first + n, 0], -1.0,
                                               rstd[:, first:first + n], ALU.mult, ALU.mult).then_inc(nm, 1)

            def stats1(turn, chunk=None):
                first, n = LN1[turn]
                for ch in range(first, first + n) if chunk is None else [chunk]:
                    dve.wait_ge(s_x[min(ch, 2)], 16 * Q)
                    for i in range(ch * TI, ch * TI + TI):
                        last = nc.vector.bn_stats(stat1[:, i, :], xs[:, i, :])
                if ch == first + n - 1:
                    last.then_inc(s_bn, 1)

            def means1(turn):
                first, n = LN1[turn]
                means(stat1, mv1, veps1, first * TI, n * TI, s_bn, s_ag, s_ve, turn + 1)

            def shifts1(turn):
                first, n = LN1[turn]
                shifts(mv1, rstd1, nmr1, first * TI, n * TI, s_rs1, s_nm1, turn + 1)

            def x_of(c, i=0, n=TI):
                k, r = c
                return xs[:, bass.ds(k * (2 * TI) + (r * TI + i), n), :].rearrange("p i d -> p (i d)")

            def add_cross(c):
                dve.wait_ge(s_att, count(c, 1, 1))
                if c[1] > 0:
                    dve.wait_ge(s_xn, count(c, 2, 2))
                nc.vector.scalar_tensor_tensor(x_of(c), att[:, :], tg[:, 0:1], x_of(c), ALU.mult, ALU.add)\
                  .then_inc(s_x1, 1)

            def stats2_of(c, i0):
                for i in (i0, i0 + 1):
                    last = nc.vector.bn_stats(stats2[:, i, :], x_of(c, i, 1))
                last.then_inc(s_bn2, 1)

            def lo_x2(c):
                p = c[1] % 2
                dve.wait_ge(s_x2h, count(c, 1, 1))
                nc.vector.tensor_tensor(x2l[p][:, :], tp[:, :], x2h[p][:, :].bitcast(F32),
                                        ALU.subtract).then_inc(s_x2l, 1)

            def over_experts(a):
                return a[:, :].unsqueeze(2).to_broadcast([P, TI, E])

            def shift_logits(c):
                dve.wait_ge(s_lg, count(c, 1, 1))
                if c[1] > 0:
                    dve.wait_ge(s_exp, count(c, 1))
                parts = misc[:, 0:TI * 2 * NE].rearrange("p (i h e) -> p i h e", i=TI, h=2)
                nc.vector.tensor_tensor(lg[:, :, :], parts[:, :, 0, 0:E],
                                        rb[:, :].unsqueeze(1).to_broadcast([P, TI, E]), ALU.add).then_inc(s_lb, 1)
                dve.wait_ge(s_lb, count(c, 2, 1))
                nc.vector.tensor_tensor(lg[:, :, :], lg[:, :, :], parts[:, :, 1, 0:E], ALU.add).then_inc(s_lb, 1)
                dve.wait_ge(s_lb, count(c, 2, 2))
                nc.vector.reduce_max(mx[:, :], lg[:, :, :], AX.X).then_inc(s_mx, 1)
                dve.wait_ge(s_mx, count(c, 1, 1))
                nc.vector.tensor_tensor(lg[:, :, :], lg[:, :, :], over_experts(mx), ALU.subtract).then_inc(s_sub, 1)

            def probabilities(c):
                dve.wait_ge(s_exp, count(c, 1, 1))
                nc.vector.reduce_sum(sm[:, :], ex[:, :, :], AX.X).then_inc(s_sm, 1)
                dve.wait_ge(s_sm, count(c, 1, 1))
                nc.vector.reciprocal(rs[:, :], sm[:, :]).then_inc(s_rc, 1)
                dve.wait_ge(s_rc, count(c, 1, 1))
                nc.vector.tensor_tensor(pr[:, :, 0:E], ex[:, :, :], over_experts(rs), ALU.mult).then_inc(s_pr, 1)

            def top_three(c):
                dve.wait_ge(s_fill, 2)
                dve.wait_ge(s_pr, count(c, 1, 1))
                for i in range(TI):
                    last = nc.vector.max(top[:, i, :], pr[:, i, 0:E])
                last.then_inc(s_top, 1)
                dve.wait_ge(s_top, count(c, 1, 1))
                nc.vector.memset(top[:, :, TOPK:8], -1.0).then_inc(s_low, 1)
                dve.wait_ge(s_fill, 2)
                dve.wait_ge(s_low, count(c, 1, 1))
                for i in range(TI):
                    last = nc.vector.match_replace(rest[:, i, :], top[:, i, :], pr[:, i, :], 0.0)
                last.then_inc(s_mr, 1)

            def gates(c):
                dve.wait_ge(s_mr, count(c, 1, 1))
                if c[1] > 0:
                    dve.wait_ge(s_t3, count(c, 1))
                nc.vector.tensor_tensor(cw[:, :, 3, 0:E], pr[:, :, 0:E], rest[:, :, 0:E], ALU.subtract).then_inc(s_cwf, 1)
                dve.wait_ge(s_cwf, count(c, 1, 1))
                for b in range(2):
                    last = nc.vector.tensor_copy(cw[:, :, b, 0:E].bitcast(F32R), cw[:, :, 3, 0:E])
                last.then_inc(s_cwh, 1)
                dve.wait_ge(s_cwh, count(c, 1, 1))
                nc.vector.tensor_tensor(cw[:, :, 2, 0:E].bitcast(F32R), cw[:, :, 3, 0:E], cw[:, :, 0, 0:E], ALU.subtract)\
                  .then_inc(s_cw, 1)

            def add_y(c):
                k, r = c
                p = r % 2
                dve.wait_ge(s_t4, count(c, 1, 1))
                if r >= 2:
                    dve.wait_ge(s_out[p], count_slot(before(c, 2), 16 * Q))
                nc.vector.scalar_tensor_tensor(ob[p][:, :, :].rearrange("p i d -> p (i d)"), misc[:, :], tg[:, 1:2],
                                               x_of(c), ALU.mult, ALU.add).then_inc(s_fin, 1)

            def scale(c, u):
                n = u % NT
                k, r = c
                dve.wait_ge(s_z, count(c, NE, u + 1))
                if r > 0 or u >= NT:
                    v = (u - NT) % NE
                    of = c if u >= NT else before(c)
                    dve.wait_ge(s_hi, count(c, NE, u + 1 - NT))
                    if v in POOL_LO:
                        dve.wait_ge(s_loP, lo_count(of, v, POOL_LO))
                    else:
                        dve.wait_ge(s_loD, lo_count(of, v, DVE_LO))
                if u == 0:
                    nc.vector.tensor_scalar(t[n], z[u % NZ][:, :], nb1T[:, 0:1], None, ALU.max).then_inc(s_a, 1)
                    return
                for g, es in enumerate(GROUP):
                    if es[0] == u - 1:
                        if g >= DIRECT:
                            dve.wait_ge(s_cwb[g], count(c, 16, 16))
                        elif c[1] > 0:
                            dve.wait_ge(s_cwb[g], count(c, 16))
                if c[1] == 0 and u - 1 in DIRECTLY:
                    dve.wait_ge(s_bcc, u)
                nc.vector.scalar_tensor_tensor(t[n], z[u % NZ][:, :], nb1T[:, u:u + 1],
                                               cwB[:, u - 1, :], ALU.max, ALU.mult).then_inc(s_a, 1)

            def low(c, u):
                n = u % NT
                dve.wait_ge(s_hi, count(c, NE, u + 1))
                if c[1] > 0 or u >= NT:
                    dve.wait_ge(s_h2, count(c, NE, u + 1 - NT))
                nc.vector.tensor_tensor(tl[n][:, :], t[n], th[n][:, :].bitcast(F32),
                                        ALU.subtract).then_inc(s_loD, 1)

            def aggregate2(c, turn):
                dve.wait_ge(s_fill, 2)
                dve.wait_ge(s_bn2, turn)
                for i in range(TI):
                    last = nc.vector.bn_aggr(mv2[:, i, :], stats2[:, i, :])
                last.then_inc(s_ag2, 1)
                dve.wait_ge(s_ag2, count(c, 1, 1))
                nc.vector.tensor_scalar_add(veps2[:, :], mv2[:, :, 1], EPS).then_inc(s_ve2, 1)

            def experts(c, todo):
                turn = 0
                spaced = SPACED
                for u in range(NE):
                    for f, at in todo:
                        if at.get("S2") == u:
                            turn = held(dve, f"ln2_turn{f[1]}", count(f, 2, 2))
                            if at["AX"] < u:
                                dve.wait_ge(s_x1, count(f, 1, 1))
                    scale(c, u)
                    if u - 1 in DVE_LO:
                        low(c, u - 1)
                    for late, at in LATE.items() if c[1] == 0 else ():
                        if u in at["stats"]:
                            stats1(late, LN1[late][0] + at["stats"].index(u))
                        if u == at["mean"]:
                            means1(late)
                        if u == at["shift"]:
                            shifts1(late)
                    for f, at in todo:
                        if at.get("AX") == u:
                            add_cross(f)
                            if at["S2"] == u:
                                dve.wait_ge(s_x1, count(f, 1, 1))
                        if at.get("S2") == u:
                            stats2_of(f, 0)
                        if at.get("S2") == u - 1:
                            stats2_of(f, 2)
                            aggregate2(f, turn)
                        if at.get("NM") == u:
                            shifts(mv2, rstd2, nmr2, 0, TI, s_rs2, s_nm2, count(f, 1, 1))
                        if at.get("LO") == u:
                            lo_x2(f)
                        if at.get("SH") == u:
                            shift_logits(f)
                        for n, part in enumerate((probabilities, top_three, gates)):
                            if at.get("CH") == u - n * spaced:
                                part(f)
                    if u == AY and c[1] > 0:
                        add_y(before(c))
                if NE - 1 in DVE_LO:
                    low(c, NE - 1)

            dve.wait_ge(s_idx, 16)
            nc.vector.tensor_scalar(idx_neg[:, :], idx_raw[:, :], 0.0, float(NMAT), ALU.is_lt, ALU.mult).then_inc(s_idv, 1)
            dve.wait_ge(s_idv, 1)
            nc.vector.tensor_tensor(idx_raw[:, :], idx_raw[:, :], idx_neg[:, :], ALU.add).then_inc(s_idv, 1)
            dve.wait_ge(s_idv, 2)
            nc.vector.tensor_scalar(idx[:, :], idx_raw[:, :], 0.0, float(NMAT - 1), ALU.max, ALU.min).then_inc(s_idxok, 1)
            def copy_ctx(m):
                dve.wait_ge(s_ctp, m + 1)
                nc.vector.tensor_copy(ctxT[:, m * TI:(m + 1) * TI, :].rearrange("p m o -> p (m o)"), z[m % NZ][:, :])\
                  .then_inc(s_ctD, 1)

            stats1(0)
            means1(0)
            for m in range(1, CTX_DVE, 2):
                copy_ctx(m)
            shifts1(0)
            for m in range(CTX_DVE + 1, NMAT // TI, 2):
                copy_ctx(m)
            nc.vector.memset(rW[:, E:NE], 0.0).then_inc(s_rwpad, 1)
            dve.wait_ge(s_rwpad, 1)
            dve.wait_ge(s_rw, 32)
            nc.vector.tensor_copy(rWs[:, 0, :], rW[:, :]).then_inc(s_wrest, 1)
            dve.wait_ge(s_wrest, 1)
            nc.vector.tensor_tensor(rWs[:, 1, :], rW[:, :], rWs[:, 0, :].bitcast(F32), ALU.subtract).then_inc(s_wrest, 1)
            dve.wait_ge(s_b1T, 1)
            nc.vector.tensor_copy(bT[:, :, :].rearrange("p b e -> p (b e)"), misc[:, 0:2 * NE]).then_inc(s_b1c, 1)
            nc.vector.tensor_scalar(nb1T[:, 0:1], misc[:, E:NE], -1.0, None, ALU.mult)
            nc.vector.tensor_scalar(nb1T[:, 1:NE], misc[:, 0:E], -1.0, None, ALU.mult).then_inc(s_b1c, 1)
            stats1(1)
            means1(1)

            def lo_w1(m):
                dve.wait_ge(s_whi, m + 1)
                sl = slice(m * NE // 2, (m + 1) * NE // 2)
                nc.vector.tensor_tensor(W1l[:, sl, :], W1n[:, sl, :], W1h[:, sl, :].bitcast(F32),
                                        ALU.subtract).then_inc(s_wlo, 1)

            lo_w1(0)
            shifts1(1)
            dve.wait_ge(s_tg, 1)
            dve.wait_ge(s_xn, 2)
            add_cross((0, 0))
            dve.wait_ge(s_x1, 1)
            stats2_of((0, 0), 0)
            stats2_of((0, 0), 2)
            aggregate2((0, 0), 2)
            shifts(mv2, rstd2, nmr2, 0, TI, s_rs2, s_nm2, 1)
            lo_w1(1)
            dve.wait_ge(s_off, 1)
            nc.vector.tensor_tensor(offT[:, :], z[NZ - 1][:, 0:NE], bT[:, 1, :], ALU.add).then_inc(s_off2, 1)
            dve.wait_ge(s_off2, 1)
            dve.wait_ge(s_zero, 1)
            nc.vector.tensor_copy(offX[:, 0, 0:NE].bitcast(F32R), offT[:, :])
            nc.vector.tensor_copy(offX[:, 2, 0:NE].bitcast(F32R), offT[:, :]).then_inc(s_offh, 1)
            dve.wait_ge(s_offh, 1)
            nc.vector.tensor_tensor(offX[:, 1, 0:NE].bitcast(F32R), offT[:, :], offX[:, 0, 0:NE], ALU.subtract)\
              .then_inc(s_offc, 1)
            stats1(2)
            lo_x2((0, 0))
            means1(2)
            dve.wait_ge(s_fill, 2)
            shift_logits((0, 0))
            dve.wait_ge(s_offT, 1)
            nc.vector.tensor_copy(offS[:, :], z[NZ - 1][0:2 * BW + NE, 0:P]).then_inc(s_offr, 1)
            probabilities((0, 0))
            top_three((0, 0))
            gates((0, 0))
            add_cross((0, 1))
            dve.wait_ge(s_x1, 2)
            stats2_of((0, 1), 0)
            stats2_of((0, 1), 2)
            aggregate2((0, 1), 4)
            shifts1(2)
            experts((0, 0), plan((0, 0)))
            with dve.Fori(0, LOOPS) as k:
                for r in (1, 2):
                    experts((k, r), plan((k, r)))
            for n, c in enumerate(TAIL):
                experts(c, plan(c, len(TAIL) - n))
            add_y(c)


_INS = ['x', 'itok_S_0_31', 'ctx_1024', 'g_xattn', 'g_ffn', 'L0_ffn_router_W', 'L0_ffn_router_b', 'L0_ffn_sW1',
        'L0_ffn_sb1', 'L0_ffn_sW2', 'L0_ffn_sb2', 'L0_ffn_eW1', 'L0_ffn_eb1', 'L0_ffn_eW2', 'L0_ffn_eb2']


def kernel(**inputs):
    import numpy as _np
    import concourse.bacc as _bacc
    from concourse import mybir as _mybir
    from concourse.bass_utils import run_bass_kernel_spmd as _run

    nc = _bacc.Bacc("TRN2", target_bir_lowering=False, num_devices=1)
    arrays, args = {}, []
    for name in _INS:
        a = _np.ascontiguousarray(inputs[name])
        arrays[f"in_{name}"] = a
        args.append(nc.dram_tensor(f"in_{name}", a.shape, _mybir.dt.from_np(a.dtype), kind="ExternalInput").ap())
    x = arrays["in_x"]
    out = nc.dram_tensor("out_dram", x.shape, _mybir.dt.from_np(x.dtype), kind="ExternalOutput").ap()
    gated_moe_block(nc, *args, out)
    r = _run(nc, [arrays], core_ids=[0])
    return r.results[0]["out_dram"]
```
